# Optimizing a Trainium2 kernel written in Bass

```python
import numpy as np
import jax
import jax.numpy as jnp

def _softmax(x, axis=-1):
    return jax.nn.softmax(x, axis=axis)

def _gelu(x):
    return jax.nn.gelu(x, approximate=True)

def _silu(x):
    return jax.nn.silu(x)

def _sigmoid(x):
    return jax.nn.sigmoid(x)

def _layernorm(x, axis=-1, eps=1e-05):
    m = jnp.mean(x, axis=axis, keepdims=True)
    v = jnp.var(x, axis=axis, keepdims=True)
    return (x - m) / jnp.sqrt(v + eps)

def _scatter_add(tgt, idx, src, axis=0):
    return tgt.at[idx].add(src)

def _segment_sum(src, seg, n):
    return jax.ops.segment_sum(src, seg, n)
kernel_name = 'mk_xattn_ffn_d1_seqx_r8_6a6c9f'

def setup_inputs(seed: int=0):
    np.random.seed(seed)
    _w = jnp.asarray

    def _rec_inputs():
        import jax
        import jax.numpy as jnp
        _rk = jax.random.key(seed)
        x = -0.0003929 + 0.9999 * jax.random.normal(jax.random.fold_in(_rk, 1), (16, 256, 128), jnp.float32)
        _lenS = 256 - jax.random.randint(jax.random.fold_in(_rk, 7), (16,), 0, max(1, 256 // 4) + 1, jnp.int32)
        _lenS2 = 1601 - jax.random.randint(jax.random.fold_in(_rk, 8), (16,), 0, max(1, 1601 // 4) + 1, jnp.int32)
        _ctx_1024P = jax.random.normal(jax.random.fold_in(_rk, 11), (16, 16, 128), jnp.float32)
        _ctx_1024c = jax.random.dirichlet(jax.random.fold_in(_rk, 511), 0.3 * jnp.ones((16,), jnp.float32), (16, 1601))
        _ctx_1024t = jnp.einsum('bsk,bkd->bsd', _ctx_1024c, _ctx_1024P)
        _ctx_1024t = _ctx_1024t * jax.lax.rsqrt(jnp.mean(jnp.square(_ctx_1024t)) + 1e-12) * 0.953939
        ctx_1024 = 2.81802e-05 + 1.00001 * (_ctx_1024t + 0.3 * jax.random.normal(jax.random.fold_in(_rk, 611), (16, 1601, 128), jnp.float32))
        _validS = jnp.arange(256)[None, :] < _lenS[:, None]
        _validS2 = jnp.arange(1601)[None, :] < _lenS2[:, None]
        _causal = jnp.tril(jnp.ones((256, 256), dtype=bool))
        mask_BxS2_ik0 = jnp.where(jnp.broadcast_to(_validS2[:, :], (16, 1601)), 0, 1).astype(jnp.int32)
        return (x, ctx_1024, mask_BxS2_ik0)
    x, ctx_1024, mask_BxS2_ik0 = _rec_inputs()

    def _L0_xattn_setup():
        import jax, jax.numpy as jnp
        import numpy as np
        D = 128
        NEG = -1000000000.0
        key = jax.random.key(seed)
        ks = jax.random.split(key, 9)
        B, Lq, Lk, d = (8, 256, 256, D)
        s = 1.0 / np.sqrt(d)
        return {'hm_tokens': jax.random.normal(ks[0], (B, Lq, d), jnp.float32), 'text_tokens': jax.random.normal(ks[1], (B, Lk, d), jnp.float32), 'text_mask': jax.random.randint(ks[2], (B, Lk), 0, 2, jnp.int32), 'Wq': jax.random.normal(ks[3], (d, d), jnp.float32) * s, 'bq': jnp.zeros((d,), jnp.float32), 'Wk': jax.random.normal(ks[4], (d, d), jnp.float32) * s, 'bk': jnp.zeros((d,), jnp.float32), 'Wv': jax.random.normal(ks[5], (d, d), jnp.float32) * s, 'bv': jnp.zeros((d,), jnp.float32)}
    _L0_xattn_all = _L0_xattn_setup()
    _L0_xattn_in = {k: v for k, v in _L0_xattn_all.items() if k in ('Wq', 'bq', 'Wk', 'bk', 'Wv', 'bv')}
    del _L0_xattn_all

    def _L0_ffn_setup():
        import jax, jax.numpy as jnp
        import numpy as np
        DIM = 128
        HIDDEN = 256
        N_EXPERTS = 8
        TOP_K = 2
        EPS = 1e-06

        def rms_norm(x, scale, eps=EPS):
            ms = jnp.mean(jnp.square(x.astype(jnp.float32)), axis=-1, keepdims=True)
            s = scale.astype(jnp.float32) * jax.lax.rsqrt(ms + eps)
            return x * s.astype(x.dtype)

        def moe_linear(xf, ids, W):
            E = W.shape[0]
            out = jnp.zeros((xf.shape[0], W.shape[1]), dtype=xf.dtype)
            for e in range(E):
                out = out + jnp.where((ids == e)[:, None], xf @ W[e].T, 0.0)
            return out
        key = jax.random.key(seed)
        k1, k2, k3, k4 = jax.random.split(key, 4)
        x = jax.random.normal(k1, (4, 512, DIM), dtype=jnp.float32)
        norm_scale = jnp.ones((DIM,), dtype=jnp.float32)
        w_router = jax.random.normal(k2, (N_EXPERTS, DIM), dtype=jnp.float32) / np.sqrt(DIM)
        lim_up = np.sqrt(6.0 / (DIM + 2 * HIDDEN))
        w_up = jax.random.uniform(k3, (N_EXPERTS, 2 * HIDDEN, DIM), dtype=jnp.float32, minval=-lim_up, maxval=lim_up)
        lim_dn = np.sqrt(6.0 / (HIDDEN + DIM))
        w_down = jax.random.uniform(k4, (N_EXPERTS, DIM, HIDDEN), dtype=jnp.float32, minval=-lim_dn, maxval=lim_dn)
        return {'x': x, 'norm_scale': norm_scale, 'w_router': w_router, 'w_up': w_up, 'w_down': w_down}
    _L0_ffn_all = _L0_ffn_setup()
    _L0_ffn_in = {k: v for k, v in _L0_ffn_all.items() if k in ('norm_scale', 'w_router', 'w_up', 'w_down')}
    del _L0_ffn_all
    return {'x': x, 'ctx_1024': ctx_1024, 'mask_BxS2_ik0': mask_BxS2_ik0, 'L0_xattn_Wq': _L0_xattn_in['Wq'], 'L0_xattn_bq': _L0_xattn_in['bq'], 'L0_xattn_Wk': _L0_xattn_in['Wk'], 'L0_xattn_bk': _L0_xattn_in['bk'], 'L0_xattn_Wv': _L0_xattn_in['Wv'], 'L0_xattn_bv': _L0_xattn_in['bv'], 'L0_ffn_norm_scale': _L0_ffn_in['norm_scale'], 'L0_ffn_w_router': _L0_ffn_in['w_router'], 'L0_ffn_w_up': _L0_ffn_in['w_up'], 'L0_ffn_w_down': _L0_ffn_in['w_down']}

def reference(x, ctx_1024, mask_BxS2_ik0, L0_xattn_Wq, L0_xattn_bq, L0_xattn_Wk, L0_xattn_bk, L0_xattn_Wv, L0_xattn_bv, L0_ffn_norm_scale, L0_ffn_w_router, L0_ffn_w_up, L0_ffn_w_down):
    import jax
    import jax.numpy as jnp

    def _L0_xattn_ref(hm_tokens, text_tokens, text_mask, Wq, bq, Wk, bk, Wv, bv):
        import jax, jax.numpy as jnp
        import numpy as np
        D = 128
        NEG = -1000000000.0
        d = hm_tokens.shape[-1]
        Q = hm_tokens @ Wq + bq
        K = text_tokens @ Wk + bk
        V = text_tokens @ Wv + bv
        scores = jnp.einsum('bqd,bkd->bqk', Q, K) / jnp.sqrt(jnp.float32(d))
        scores = jnp.where(text_mask[:, None, :] == 0, jnp.float32(NEG), scores)
        attn = jax.nn.softmax(scores, axis=-1)
        return jnp.einsum('bqk,bkd->bqd', attn, V)

    def _L0_ffn_ref(x, norm_scale, w_router, w_up, w_down):
        import jax, jax.numpy as jnp
        import numpy as np
        DIM = 128
        HIDDEN = 256
        N_EXPERTS = 8
        TOP_K = 2
        EPS = 1e-06

        def rms_norm(x, scale, eps=EPS):
            ms = jnp.mean(jnp.square(x.astype(jnp.float32)), axis=-1, keepdims=True)
            s = scale.astype(jnp.float32) * jax.lax.rsqrt(ms + eps)
            return x * s.astype(x.dtype)

        def moe_linear(xf, ids, W):
            E = W.shape[0]
            out = jnp.zeros((xf.shape[0], W.shape[1]), dtype=xf.dtype)
            for e in range(E):
                out = out + jnp.where((ids == e)[:, None], xf @ W[e].T, 0.0)
            return out
        B, S, D = x.shape
        skip = x
        xn = rms_norm(x, norm_scale)
        scores = (xn @ w_router.T).astype(jnp.float32)
        scores_topk, idx = jax.lax.top_k(scores, TOP_K)
        weights = jax.nn.softmax(scores_topk, axis=-1)
        xf = jnp.broadcast_to(xn[..., None, :], (B, S, TOP_K, D)).reshape(-1, D)
        ids = idx.reshape(-1)
        up = moe_linear(xf, ids, w_up)
        u, gate = jnp.split(up, 2, axis=-1)
        h = u * jax.nn.silu(gate)
        down = moe_linear(h, ids, w_down)
        down = down.reshape(B, S, TOP_K, D)
        out = jnp.sum(down * weights[..., None].astype(down.dtype), axis=-2)
        return out + skip
    x = x + _L0_xattn_ref(_layernorm(x, axis=-1), ctx_1024, mask_BxS2_ik0, L0_xattn_Wq, L0_xattn_bq, L0_xattn_Wk, L0_xattn_bk, L0_xattn_Wv, L0_xattn_bv)
    x = x + _L0_ffn_ref(_layernorm(x, axis=-1), L0_ffn_norm_scale, L0_ffn_w_router, L0_ffn_w_up, L0_ffn_w_down)
    return x

_drawn_inputs = setup_inputs


def setup_inputs(seed=0):
    import zlib

    import numpy as np

    out = dict(_drawn_inputs(seed))
    spreads = {'L0_xattn_bq': (0.0, 0.357),
     'L0_xattn_bk': (0.0, 0.8),
     'L0_xattn_bv': (0.0, 0.1),
     'L0_ffn_norm_scale': (1.0, 0.2)}
    factors = {}
    for name, (base, spread) in spreads.items():
        noise = np.random.default_rng([zlib.crc32(name.encode()), seed]).standard_normal(out[name].shape)
        drawn = base * np.exp(spread * noise) if base else spread * noise
        out[name] = jnp.asarray(drawn.astype(out[name].dtype))
    for name, factor in factors.items():
        out[name] = (out[name] * factor).astype(out[name].dtype)
    return out
```

```python
from contextlib import ExitStack

import concourse.bass as bass
from concourse import mybir

F32 = mybir.dt.float32
I32 = mybir.dt.int32
U32 = mybir.dt.uint32
ALU = mybir.AluOpType
ACT = mybir.ActivationFunctionType
AX = mybir.AxisListType

P = 128
LN_EPS = 1e-5
RMS_EPS = 1e-6
MASKED = -1e30
LOWEST = -3.4e38
BANK = 512


def wait(eng, sem, value):
    if not isinstance(value, int) or value > 0:
        eng.wait_ge(sem, value)


def xattn_moe(nc, x, ctx_rows, ctx_cols, mask, wq, wk_t, wv, bq, bk, bv, norm_scale, w_router_t,
              w_up_t, w_down_t, out):
    B, SQ, D = x.shape
    SK = ctx_rows.shape[1]
    E, _, H2 = w_up_t.shape
    H = H2 // 2
    QT = SQ // P
    UNITS = B * QT
    TOK = B * SQ
    KT = -(-SK // P)
    TAIL = SK - (KT - 1) * P
    GROUPS = -(-KT // 4)
    HC = H // P
    SCALE = float(D) ** -0.5
    assert D == P and QT == 2 and B % 2 == 0 and B >= 6 and GROUPS == 4 and TAIL < P and HC == 2 and E == 8
    PAIRS = B // 2
    RING = 4
    TOP_K = 2
    GROUPS_D = 2
    GU = UNITS // GROUPS_D
    GB = TOP_K * GU + E
    NB = GROUPS_D * GB
    CH = 4
    SB = 2 * CH
    GC = GB // CH
    SPLIT = GU // 4 + 1
    assert GB % SB == 0 and GU % 4 == 0 and 1 < SPLIT < PAIRS - 1

    def batch_part(t):
        return P if t < KT - 1 else TAIL

    x_tiles = x.rearrange("b (t p) d -> b p t d", p=P)
    out_tiles = out.rearrange("b (t p) d -> p (b t) d", p=P)

    rows_in = [nc.dram_tensor(f"rows_in{g}", [GB * P, D], F32, kind="Internal").ap() for g in range(GROUPS_D)]
    rows_out = [nc.dram_tensor(f"rows_out{g}", [GB * P, D], F32, kind="Internal").ap() for g in range(GROUPS_D)]
    mbias_dram = nc.dram_tensor("mbias_dram", [B, SK], F32, kind="Internal").ap()

    st = ExitStack()
    with st:
        def sb(name, shape, dt=F32):
            return st.enter_context(nc.sbuf_tensor(name, shape, dt))

        def sem(name):
            return st.enter_context(nc.semaphore(name))

        wq_sb = sb("wq_sb", [P, D])
        wkt_sb = sb("wkt_sb", [P, D])
        wv_sb = sb("wv_sb", [P, D])
        wr_sb = sb("wr_sb", [P, E])
        wup_sb = sb("wup_sb", [P, E, H2])
        wdn_sb = sb("wdn_sb", [P, E, HC, D])
        bq_col = sb("bq_col", [P, 1])
        bk_col = sb("bk_col", [P, 1])
        bv_rows = sb("bv_rows", [P, D])
        norm_rows = sb("norm_rows", [P, D])
        ident = sb("ident", [P, P])
        spare = sb("spare", [P, 1])
        minus_half = sb("minus_half", [P, QT])
        iota_i = sb("iota_i", [P, E], I32)
        iota_f = sb("iota_f", [P, E])
        x_in = sb("x_in", [P, 2, QT, D])
        xn1 = sb("xn1", [P, 2, QT, D])
        ctx_sb = sb("ctx_sb", [P, 2, KT, D])
        ctxt_sb = sb("ctxt_sb", [P, 2, SK])
        mask_i = sb("mask_i", [B, SK], I32)
        mbias_rows = sb("mbias_rows", [B, SK])
        mbias = sb("mbias", [P, 2, SK])
        xt_sb = sb("xt_sb", [P, SQ])
        qt_sb = sb("qt_sb", [P, SQ])
        gt_sb = sb("gt_sb", [P, 2, SQ])
        qbk = sb("qbk", [P, 2, QT])
        st1 = sb("st1", [P, QT, 6])
        mv1 = sb("mv1", [P, QT, 2])
        ve1 = sb("ve1", [P, QT])
        rstd1 = sb("rstd1", [P, QT])
        scores = sb("scores", [P, 2, SK])
        probs = sb("probs", [P, 2, SK])
        probs_t = sb("probs_t", [P, 2, KT * P])
        smax = sb("smax", [P, RING])
        smax2 = sb("smax2", [P, RING])
        ebias = sb("ebias", [P, RING])
        esum = sb("esum", [P, RING])
        rsum = sb("rsum", [P, RING])
        o_t = sb("o_t", [P, 2, P])
        x1 = sb("x1", [P, RING, D])
        st2 = sb("st2", [P, 6])
        mv2 = sb("mv2", [P, 2])
        ve2 = sb("ve2", [P, 1])
        ms = sb("ms", [P, 1])
        rstd2 = sb("rstd2", [P, 1])
        y = sb("y", [P, 2, D])
        ysq = sb("ysq", [P, D])
        ss = sb("ss", [P, 1])
        rrms = sb("rrms", [P, 1])
        xn2 = sb("xn2", [P, 2, D])
        xnt = sb("xnt", [P, 2, P])
        logits = sb("logits", [P, E])
        top = sb("top", [P, 8])
        top_i = sb("top_i", [P, 8], U32)
        top_f = sb("top_f", [P, 2, 2])
        sdiff = sb("sdiff", [P, 1])
        e2 = sb("e2", [P, 2, 1])
        den = sb("den", [P, 1])
        hot = sb("hot", [P, TOP_K, UNITS, E])
        gate_all = sb("gate_all", [P, UNITS, TOP_K])
        xn2_all = sb("xn2_all", [P, UNITS, D])
        base_all = sb("base_all", [P, UNITS, D])
        place = sb("place", [P, TOP_K, UNITS], I32)
        ones = sb("ones", [P, P])
        before = sb("before", [P, P])
        zeros = sb("zeros", [P, D])
        keep = sb("keep", [P, E, GU])
        count_i = sb("count_i", [P, GB], I32)
        count_f = sb("count_f", [P, GB])
        rows128 = sb("rows128", [P, GU])
        chosen = sb("chosen", [P, GU, E])
        rank = sb("rank", [P, GU, E])
        total = sb("total", [P, E, GU])
        upto = sb("upto", [P, E, GU])
        filled = sb("filled", [P, E, GU])
        blocks = sb("blocks", [P, E])
        blocks_end = sb("blocks_end", [P, E])
        first = sb("first", [P, E, GU])
        spot = sb("spot", [P, GU, E])
        spot_k = sb("spot_k", [P, TOP_K, GU, E])
        place_f = sb("place_f", [P, TOP_K, GU])
        past = sb("past", [P, GB, E])
        owner_f = sb("owner_f", [P, GB])
        owner = sb("owner", [P, NB], I32)
        blk_x = sb("blk_x", [P, 2, CH, D])
        blk_xt = sb("blk_xt", [P, 2, P])
        th = sb("th", [P, 2, H])
        sg = sb("sg", [P, 2, H])
        hid = sb("hid", [P, 2, H])
        hid_t = sb("hid_t", [P, 2, HC * P])
        blk_y = sb("blk_y", [P, 2, CH, D])
        got = sb("got", [P, GU, TOP_K, D])

        ps = st.enter_context(nc.psum_tensor("ps", [P, 8, BANK], F32))
        ps_scores = ps[:, 0:4, :].rearrange("p a b -> p (a b)")
        ps_turn = ps[:, 4:6, :]
        ps_o = ps[:, 6, :]
        ps_misc = ps[:, 7, :]

        s_consts = sem("consts_loaded")
        s_experts = sem("experts_loaded")
        s_mbias = [sem(f"mbias_loaded{j}") for j in range(2)]
        s_x = [sem(f"x_loaded{j}") for j in range(2)]
        s_ctx = [sem(f"ctx_loaded{j}") for j in range(2)]
        s_ctxt = [sem(f"ctxt_loaded{j}") for j in range(2)]
        s_mask = sem("mask_loaded")
        s_mrows = sem("mask_bias_made")
        s_mstore = sem("mask_bias_stored")
        s_stored = sem("stored")
        s_cleared = sem("rows_cleared")
        s_blk = [sem(f"block_rows_loaded{j}") for j in range(2)]
        s_ybuf = [sem(f"result_buffer_stored{j}") for j in range(2)]
        s_scat = [sem(f"rows_scattered{g}") for g in range(GROUPS_D)]
        s_got = [sem(f"rows_gathered{n}") for n in range(GU)]
        s_pool = sem("pool_consts_set")
        s_ident = sem("ident_ready")
        s_xb = sem("x_plus_bv_ready")
        s_base = sem("base_ready")
        s_keep = sem("xn2_kept")
        s_zeros = sem("zeros_set")
        s_tables = sem("dispatch_tables_set")
        s_scores = sem("scores_ready")
        s_turned = sem("probs_turned")
        s_pv = sem("pv_done")
        s_attn = sem("attn_ready")
        s_xt = sem("xt_ready")
        s_qt = sem("qt_ready")
        s_gt = sem("gt_ready")
        s_rt = sem("rt_ready")
        s_logits = sem("logits_ready")
        s_rank = sem("rank_ready")
        s_bxt = sem("block_turned")
        s_up = sem("up_ready")
        s_ht = sem("hidden_turned")
        s_down = sem("down_ready")
        s_exp = sem("exp_done")
        s_pt_act = sem("probs_t_by_act")
        s_ot = sem("o_t_ready")
        s_xtc = sem("xt_copied")
        s_qtc = sem("qt_copied")
        s_rtc = sem("rt_copied")
        s_e2 = sem("e2_ready")
        s_bxc = sem("block_turned_copied")
        s_htc = sem("hidden_turned_copied")
        s_th = sem("tanh_ready")
        s_iota = sem("iota_ready")
        s_max = sem("max_done")
        s_max2 = sem("max2_done")
        s_ebias = sem("ebias_ready")
        s_gtc = sem("gt_copied")
        s_qbk = sem("qbk_copied")
        s_pt_dve = sem("probs_t_by_dve")
        s_rsum = sem("rsum_ready")
        s_x1 = sem("x1_ready")
        s_st1 = sem("ln1_stats")
        s_mv1 = sem("ln1_moments")
        s_ve1 = sem("ln1_var_eps")
        s_rs1 = sem("ln1_rstd")
        s_xn1 = sem("xn1_ready")
        s_st2 = sem("ln2_stats")
        s_mv2 = sem("ln2_moments")
        s_ve2 = sem("ln2_var_eps")
        s_ms = sem("mean_square_ready")
        s_rs2 = sem("ln2_rstd")
        s_y = sem("y_ready")
        s_ss = sem("ss_ready")
        s_rr = sem("rrms_ready")
        s_xn2 = sem("xn2_ready")
        s_lg = sem("logits_copied")
        s_top = sem("top_ready")
        s_topi = sem("top_index_ready")
        s_sd = sem("sdiff_ready")
        s_topf = sem("top_f_ready")
        s_den = sem("den_ready")
        s_w1 = sem("gate1_ready")
        s_w2 = sem("gate2_ready")
        s_hot = sem("hot_ready")
        s_gates = sem("gates_ready")
        s_sg = sem("sg_ready")
        s_h = sem("h_ready")
        s_y2 = sem("block_result_ready")
        s_plan = sem("dispatch_step")
        s_rankc = sem("rank_copied")
        s_place = sem("places_ready")
        PLAN_STEPS = 12
        s_owner = sem("owners_ready")
        s_part = sem("first_choice_added")
        s_final = sem("result_ready")

        block = st.enter_context(nc.Block())

        def is_unit(u):
            return not isinstance(u, int) or 0 <= u < UNITS

        def slots(eng, slot, between):
            for k in range(4):
                slot(0, k)
            with eng.Fori(1, SPLIT) as i:
                for k in range(4):
                    slot(i, k)
            between()
            with eng.Fori(SPLIT, PAIRS - 1) as i:
                for k in range(4):
                    slot(i, k)
            for k in range(4):
                slot(PAIRS - 1, k)
            for k in range(4):
                slot(PAIRS, k)

        def is_block(m):
            return not isinstance(m, int) or 0 <= m < NB

        def steps(eng, step):
            for k in range(SB):
                step(0, k)
            with eng.Fori(1, NB // SB - 1) as i:
                for k in range(SB):
                    step(i, k)
            for k in range(SB):
                step(NB // SB - 1, k)
            for k in range(2):
                step(NB // SB, k)

        def shift(i, k, d, n):
            return (i, k + d) if 0 <= k + d < n else (i + (1 if d > 0 else -1), k + d - (n if d > 0 else -n))

        @block.sync
        def _(sp):
            def load(i, j, first=False):
                b = 2 * i + j
                wait(sp, s_xn1, b - 1)
                wait(sp, s_xb, b - 1)
                sp.dma_start(x_in[:, j], x_tiles[b]).then_inc(s_x[j], 16)
                wait(sp, s_scores, QT * (b - 1))
                sp.dma_start(ctxt_sb[:, j], ctx_cols[b]).then_inc(s_ctxt[j], 16)
                if isinstance(i, int) and b == 0:
                    sp.wait_ge(s_mstore, 16)
                wait(sp, s_max, QT * (b - 1))
                sp.dma_start(mbias[:, j], mbias_dram[b].partition_broadcast(P)).then_inc(s_mbias[j], 16)
                wait(sp, s_pv, QT * (b - 1))
                sp.dma_start(ctx_sb[:, j, 0:KT - 1],
                             ctx_rows[b][0:(KT - 1) * P].rearrange("(t p) d -> p t d", p=P)).then_inc(s_ctx[j], 16)
                sp.dma_start(ctx_sb[0:TAIL, j, KT - 1], ctx_rows[b][(KT - 1) * P:SK]).then_inc(s_ctx[j], 16)

            sp.dma_start(mask_i[:], mask).then_inc(s_mask, 16)
            for dst, src in ((wq_sb[:], wq), (wkt_sb[:], wk_t), (bq_col[:], bq), (bk_col[:], bk)):
                sp.dma_start(dst, src).then_inc(s_consts, 16)
            load(0, 0)
            for dst, src in ((wv_sb[:], wv), (wr_sb[:], w_router_t), (bv_rows[:], bv.partition_broadcast(P)),
                             (norm_rows[:], norm_scale.partition_broadcast(P))):
                sp.dma_start(dst, src).then_inc(s_consts, 16)
            load(0, 1)
            sp.dma_start(wup_sb[:], w_up_t.rearrange("e d h -> d e h")).then_inc(s_experts, 16)
            sp.dma_start(wdn_sb[:], w_down_t.rearrange("e (c p) d -> p e c d", p=P)).then_inc(s_experts, 16)
            sp.wait_ge(s_zeros, 1)
            for g in range(GROUPS_D):
                sp.dma_start(rows_in[g].rearrange("(n p) d -> p n d", p=P),
                             zeros[:].unsqueeze(1).broadcast_to([P, GB, D])).then_inc(s_cleared, 16)
            with sp.Fori(1, PAIRS) as i:
                load(i, 0)
                load(i, 1)

            in_chunks = [t.rearrange("(c t p) d -> c p t d", t=CH, p=P) for t in rows_in]
            out_chunks = [t.rearrange("(c t p) d -> c p t d", t=CH, p=P) for t in rows_out]
            GI = GC // 2

            def load_chunk(g, i2, j):
                wait(sp, s_bxt, CH * (g * GC + 2 * i2 + j - 1))
                sp.dma_start(blk_x[:, j], in_chunks[g][2 * i2 + j]).then_inc(s_blk[j], 16)

            def store_chunk(g, i2, j):
                sp.wait_ge(s_y2, CH * (g * GC + 2 * i2 + j + 1))
                sp.dma_start(out_chunks[g][2 * i2 + j], blk_y[:, j]).then_inc(s_ybuf[j], 16)

            for g in range(GROUPS_D):
                sp.wait_ge(s_scat[g], 16 * TOP_K * GU)
                for j in range(2):
                    load_chunk(g, 0, j)
                    if g:
                        store_chunk(g - 1, GI - 1, j)
                with sp.Fori(0, GI - 1) as i2:
                    for j in range(2):
                        load_chunk(g, i2 + 1, j)
                        store_chunk(g, i2, j)
            for j in range(2):
                store_chunk(GROUPS_D - 1, GI - 1, j)

            for u in range(0, UNITS, 4):
                sp.wait_ge(s_final, u + 4)
                sp.dma_start(out_tiles[:, u:u + 4], base_all[:, u:u + 4]).then_inc(s_stored, 16)
            sp.wait_ge(s_stored, 16 * UNITS // 4)

        N_CONSTS = 8 * 16

        @block.gpsimd
        def _(pool):
            def make_xb(i, j):
                b = 2 * i + j
                pool.wait_ge(s_x[j], 16 * (i + 1))
                wait(pool, s_base, QT * (b - 1))
                wait(pool, s_xn2, QT * (b - 1))
                for t in range(QT):
                    last = pool.tensor_tensor(x1[:, 2 * j + t], x_in[:, j, t], bv_rows[:], ALU.add)
                last.then_inc(s_xb, 1)

            def rstd_of_x(i, j):
                pool.wait_ge(s_ve1, 2 * i + j + 1)
                wait(pool, s_xn1, 2 * i + j)
                pool.tensor_tensor(rstd1[:], ve1[:], minus_half[:], ALU.pow).then_inc(s_rs1, 1)

            def slot(i, k):
                u = 4 * i + k
                if is_unit(u - 1):
                    pool.wait_ge(s_ve2, u)
                    wait(pool, s_y, u - 1)
                    pool.tensor_tensor(rstd2[:], ve2[:], minus_half[:, 0:1], ALU.pow).then_inc(s_rs2, 1)
                    pool.wait_ge(s_ms, u)
                    wait(pool, s_xn2, u - 1)
                    pool.tensor_tensor(rrms[:], ms[:], minus_half[:, 0:1], ALU.pow).then_inc(s_rr, 1)
                    pool.wait_ge(s_y, u)
                    pool.tensor_tensor(base_all[:, bass.ds(u - 1, 1)],
                                       x1[:, (k - 1) % 4:(k - 1) % 4 + 1], y[:, (k - 1) % 2:(k - 1) % 2 + 1],
                                       ALU.add).then_inc(s_base, 1)
                    pool.wait_ge(s_xn2, u)
                    pool.tensor_copy(xn2_all[:, bass.ds(u - 1, 1)], xn2[:, (k - 1) % 2:(k - 1) % 2 + 1]).then_inc(s_keep, 1)
                if k == 3 and is_unit(u + 1):
                    make_xb(i + 1, 0)
                if k == 1 and is_unit(u):
                    make_xb(i, 1)
                if k % 2 == 1 and is_unit(u + 3):
                    rstd_of_x(i + 1, k // 2)

            def scatter(g, n):
                u, c = g * GU + n // TOP_K, n % TOP_K
                if n == 0:
                    pool.wait_ge(s_cleared, 16 * GROUPS_D)
                    pool.wait_ge(s_place, g + 1)
                    pool.wait_ge(s_keep, GU * (g + 1))
                pool.indirect_dma_start(rows_in[g], bass.IndirectOffsetOnAxis(ap=place[:, c, u:u + 1], axis=0),
                                        xn2_all[:, u], None).then_inc(s_scat[g], 16)

            pool.memset(zeros[:], 0.0).then_inc(s_zeros, 1)
            pool.memset(ident[:], 0.0).then_inc(s_pool, 1)
            pool.memset(minus_half[:], -0.5).then_inc(s_pool, 1)
            pool.iota(iota_i[:], pattern=[[1, E]], base=0, channel_multiplier=0).then_inc(s_pool, 1)
            pool.wait_ge(s_pool, 3)
            pool.affine_select(out=ident[:], in_=ident[:], compare_op=ALU.not_equal, fill=1.0, base=0,
                               pattern=[[-1, P]], channel_multiplier=1).then_inc(s_ident, 1)
            pool.tensor_copy(iota_f[:], iota_i[:]).then_inc(s_iota, 1)
            rstd_of_x(0, 0)
            rstd_of_x(0, 1)
            pool.memset(ones[:], 1.0).then_inc(s_tables, 1)
            pool.memset(keep[:], 1.0).then_inc(s_tables, 1)
            pool.iota(count_i[:], pattern=[[1, GB]], base=0, channel_multiplier=0).then_inc(s_tables, 1)
            pool.wait_ge(s_tables, 3)
            pool.memset(keep[:, :, 0:1], 0.0).then_inc(s_tables, 1)
            pool.affine_select(out=before[:], in_=ones[:], compare_op=ALU.is_gt, fill=0.0, base=0,
                               pattern=[[1, P]], channel_multiplier=-1).then_inc(s_tables, 1)
            pool.tensor_copy(count_f[:], count_i[:]).then_inc(s_tables, 1)
            pool.wait_ge(s_tables, 6)
            pool.tensor_scalar(rows128[:], count_f[:, 0:GU], float(P), None, ALU.mult).then_inc(s_tables, 1)
            pool.wait_ge(s_consts, N_CONSTS)
            make_xb(0, 0)

            for k in range(4):
                slot(0, k)
            with pool.Fori(1, SPLIT) as i:
                for k in range(4):
                    slot(i, k)
            sent = 0
            for i in range(SPLIT, PAIRS + 1):
                for k in range(4):
                    slot(i, k)
                    for _ in range(min(3, TOP_K * GU - sent) if 4 * i + k > 4 * SPLIT else 0):
                        scatter(0, sent)
                        sent += 1
            for n in range(TOP_K * GU):
                scatter(1, n)
            for u in range(UNITS):
                g, n = u // GU, u % GU
                if n == 0:
                    for j in range(2):
                        pool.wait_ge(s_ybuf[j], 16 * (g + 1) * GC // 2)
                if g:
                    pool.wait_ge(s_final, u - GU + 1)
                for c in range(TOP_K):
                    pool.indirect_dma_start(got[:, n, c], None, rows_out[g],
                                            bass.IndirectOffsetOnAxis(ap=place[:, c, u:u + 1], axis=0)).then_inc(s_got[n], 16)

        @block.scalar
        def _(act):
            act.wait_ge(s_mrows, 1)
            act.dma_start(mbias_dram, mbias_rows[:]).then_inc(s_mstore, 16)
            act.wait_ge(s_consts, N_CONSTS)

            def prep_xt(i, j):
                b = 2 * i + j
                act.wait_ge(s_xt, b + 1)
                wait(act, s_qt, b)
                act.activation(xt_sb[:], ps_misc[:, 0:SQ], ACT.Copy).then_inc(s_xtc, 1)

            def prep_qt(i, j):
                b = 2 * i + j
                act.wait_ge(s_qt, b + 1)
                wait(act, s_gt, b)
                act.activation(qt_sb[:], ps_misc[:, 0:SQ], ACT.Identity, bias=bq_col[:]).then_inc(s_qtc, 1)

            def exp_unit(i, k):
                u = 4 * i + k
                act.wait_ge(s_ebias, u + 1)
                wait(act, s_turned, GROUPS * (u - 1))
                wait(act, s_rsum, u - 3)
                act.activation(probs[:, k % 2], scores[:, k % 2], ACT.Exp, bias=ebias[:, k:k + 1], scale=SCALE,
                               accum_out=esum[:, k:k + 1]).then_inc(s_exp, 1)

            def slot(i, k):
                u = 4 * i + k
                nxt = (i, k // 2 + 1) if k < 2 else (i + 1, 0)
                prep = k % 2 == 0 and is_unit(u + 2)
                if prep:
                    prep_xt(*nxt)
                if is_unit(u):
                    wait(act, s_pv, u - 1)
                    for g in range(GROUPS - 1):
                        if g == 2 and prep:
                            prep_qt(*nxt)
                        act.wait_ge(s_turned, GROUPS * u + g + 1)
                        act.activation(probs_t[:, k % 2, g * BANK:(g + 1) * BANK], ps_turn[:, g % 2],
                                       ACT.Copy).then_inc(s_pt_act, 1)
                if is_unit(u + 1):
                    exp_unit(*((i, k + 1) if k < 3 else (i + 1, 0)))
                if is_unit(u):
                    act.wait_ge(s_pv, u + 1)
                    wait(act, s_attn, u - 1)
                    act.activation(o_t[:, k % 2], ps_o[:, 0:P], ACT.Copy).then_inc(s_ot, 1)
                if is_unit(u - 3):
                    act.wait_ge(s_sd, u - 2)
                    wait(act, s_gates, u - 4)
                    act.activation(e2[:, (k - 3) % 2], sdiff[:], ACT.Exp).then_inc(s_e2, 1)
                if is_unit(u - 2):
                    act.wait_ge(s_rt, u - 1)
                    wait(act, s_logits, u - 3)
                    act.activation(xnt[:, k % 2], ps_misc[:, 0:P], ACT.Copy).then_inc(s_rtc, 1)

            prep_xt(0, 0)
            prep_qt(0, 0)
            exp_unit(0, 0)
            slots(act, slot, lambda: None)

            def block_xt(i, k):
                m = SB * i + k
                act.wait_ge(s_bxt, m + 1)
                wait(act, s_up, m - 1)
                act.activation(blk_xt[:, k % 2], ps[:, k % 2, 0:P], ACT.Copy).then_inc(s_bxc, 1)

            def step(i, k):
                m = SB * i + k
                if is_block(m + 1):
                    block_xt(*shift(i, k, 1, SB))
                if is_block(m):
                    act.wait_ge(s_up, m + 1)
                    wait(act, s_sg, m - 1)
                    act.activation(th[:, k % 2], ps[:, 2 + k % 2, H:H2], ACT.Tanh, scale=0.5).then_inc(s_th, 1)
                if is_block(m - 1):
                    act.wait_ge(s_ht, m)
                    wait(act, s_down, m - 2)
                    act.activation(hid_t[:, (k - 1) % 2], ps[:, 4 + (k - 1) % 2, 0:HC * P], ACT.Copy).then_inc(s_htc, 1)

            block_xt(0, 0)
            steps(act, step)

        @block.vector
        def _(dve):
            def take_waits():
                dve.memset(spare[:, 0:1], 0.0)

            def ln1(i, j):
                b = 2 * i + j
                dve.wait_ge(s_x[j], 16 * (i + 1))
                for t in range(QT):
                    last = dve.bn_stats(st1[:, t], x_in[:, j, t])
                last.then_inc(s_st1, 1)
                dve.wait_ge(s_st1, b + 1)
                take_waits()
                for t in range(QT):
                    last = dve.bn_aggr(mv1[:, t], st1[:, t])
                last.then_inc(s_mv1, 1)
                dve.wait_ge(s_mv1, b + 1)
                dve.tensor_scalar(ve1[:], mv1[:, :, 1], LN_EPS, None, ALU.add).then_inc(s_ve1, 1)
                dve.wait_ge(s_rs1, b + 1)
                wait(dve, s_xt, b - 1)
                for t in range(QT):
                    last = dve.tensor_scalar(xn1[:, j, t], x_in[:, j, t], mv1[:, t, 0:1], rstd1[:, t:t + 1],
                                             ALU.subtract, ALU.mult)
                last.then_inc(s_xn1, 1)

            def prep_gt(i, j):
                b = 2 * i + j
                dve.wait_ge(s_gt, b + 1)
                wait(dve, s_scores, QT * (b - 1))
                dve.tensor_copy(gt_sb[:, j], ps_misc[:, 0:SQ]).then_inc(s_gtc, 1)
                wait(dve, s_ebias, QT * (b - 1))
                dve.tensor_copy(qbk[:, j], ps_misc[:, SQ:SQ + QT]).then_inc(s_qbk, 1)

            def maximum(i, k):
                u = 4 * i + k
                j = k // 2
                c = qbk[:, j, k % 2:k % 2 + 1]
                dve.wait_ge(s_scores, u + 1)
                dve.wait_ge(s_mbias[j], 16 * (i + 1))
                wait(dve, s_exp, u - 1)
                take_waits()
                dve.tensor_tensor_reduce(out=scores[:, k % 2], in0=ps_scores[:, 0:SK], in1=mbias[:, j], scale=1.0,
                                         scalar=LOWEST, op0=ALU.add, op1=ALU.max,
                                         accum_out=smax[:, k:k + 1]).then_inc(s_max, 1)
                dve.wait_ge(s_max, u + 1)
                dve.wait_ge(s_qbk, 2 * i + j + 1)
                dve.tensor_scalar(smax2[:, k:k + 1], smax[:, k:k + 1], c, -SCALE, ALU.add, ALU.mult).then_inc(s_max2, 1)
                dve.wait_ge(s_max2, u + 1)
                dve.scalar_tensor_tensor(ebias[:, k:k + 1], c, SCALE, smax2[:, k:k + 1], ALU.mult,
                                         ALU.add).then_inc(s_ebias, 1)

            def post(i, k, kk):
                u = 4 * i + kk
                r = k % 4
                dve.wait_ge(s_exp, u + 1)
                dve.reciprocal(rsum[:, r:r + 1], esum[:, r:r + 1]).then_inc(s_rsum, 1)
                dve.wait_ge(s_rsum, u + 1)
                dve.wait_ge(s_attn, u + 1)
                dve.wait_ge(s_xb, (2 * i + kk // 2 + 1))
                dve.scalar_tensor_tensor(x1[:, r], ps_o[:, 0:D], rsum[:, r:r + 1], x1[:, r], ALU.mult,
                                         ALU.add).then_inc(s_x1, 1)

            def ln2(i, kk):
                u = 4 * i + kk
                r, q = kk % 4, kk % 2
                dve.wait_ge(s_x1, u + 1)
                dve.bn_stats(st2[:], x1[:, r]).then_inc(s_st2, 1)
                dve.wait_ge(s_st2, u + 1)
                take_waits()
                dve.bn_aggr(mv2[:], st2[:]).then_inc(s_mv2, 1)
                dve.wait_ge(s_mv2, u + 1)
                dve.tensor_scalar(ve2[:], mv2[:, 1:2], LN_EPS, None, ALU.add).then_inc(s_ve2, 1)
                dve.wait_ge(s_rs2, u + 1)
                wait(dve, s_base, u - 1)
                dve.tensor_scalar(y[:, q], x1[:, r], mv2[:, 0:1], rstd2[:], ALU.subtract, ALU.mult).then_inc(s_y, 1)
                dve.wait_ge(s_y, u + 1)
                dve.tensor_tensor_reduce(out=ysq[:], in0=y[:, q], in1=y[:, q], scale=1.0, scalar=0.0, op0=ALU.mult,
                                         op1=ALU.add, accum_out=ss[:]).then_inc(s_ss, 1)
                dve.wait_ge(s_ss, u + 1)
                dve.tensor_scalar(ms[:], ss[:], 1.0 / D, RMS_EPS, ALU.mult, ALU.add).then_inc(s_ms, 1)
                dve.wait_ge(s_rr, u + 1)
                wait(dve, s_rt, u - 1)
                wait(dve, s_keep, u - 1)
                dve.scalar_tensor_tensor(xn2[:, q], y[:, q], rrms[:], norm_rows[:], ALU.mult, ALU.mult).then_inc(s_xn2, 1)

            def route(i, kk):
                u = 4 * i + kk
                q = kk % 2
                dve.wait_ge(s_logits, u + 1)
                dve.tensor_copy(logits[:], ps_misc[:, 0:E]).then_inc(s_lg, 1)
                dve.wait_ge(s_lg, u + 1)
                take_waits()
                dve.max(top[:], logits[:]).then_inc(s_top, 1)
                dve.wait_ge(s_top, u + 1)
                take_waits()
                dve.max_index(top_i[:], top[:], logits[:]).then_inc(s_topi, 1)
                wait(dve, s_e2, u)
                dve.tensor_tensor(sdiff[:], top[:, 1:2], top[:, 0:1], ALU.subtract).then_inc(s_sd, 1)
                dve.wait_ge(s_topi, u + 1)
                dve.tensor_copy(top_f[:, q], top_i[:, 0:2]).then_inc(s_topf, 1)

            def gates(i, kk):
                u = 4 * i + kk
                q = kk % 2
                dve.wait_ge(s_e2, u + 1)
                dve.tensor_scalar(den[:], e2[:, q], 1.0, None, ALU.add).then_inc(s_den, 1)
                dve.wait_ge(s_topf, u + 1)
                for c in range(TOP_K):
                    dve.tensor_scalar(hot[:, c, bass.ds(u, 1)].rearrange("p a e -> p (a e)"), iota_f[:],
                                      top_f[:, q, c:c + 1], None, ALU.is_equal)
                w = gate_all[:, bass.ds(u, 1)].rearrange("p a c -> p (a c)")
                dve.wait_ge(s_den, u + 1)
                dve.reciprocal(w[:, 0:1], den[:]).then_inc(s_w1, 1)
                dve.wait_ge(s_w1, u + 1)
                dve.tensor_tensor(w[:, 1:2], w[:, 0:1], e2[:, q], ALU.mult).then_inc(s_gates, 1)

            def slot(i, k):
                u = 4 * i + k
                nxt = (i, k // 2 + 1) if k < 2 else (i + 1, 0)
                if is_unit(u - 1):
                    post(i, k - 1, k - 1)
                if is_unit(u - 3):
                    route(i, k - 3)
                if is_unit(u + 1):
                    maximum(*((i, k + 1) if k < 3 else (i + 1, 0)))
                if k % 2 == 0 and is_unit(u + 2):
                    prep_gt(*nxt)
                if is_unit(u):
                    dve.wait_ge(s_turned, GROUPS * (u + 1))
                    wait(dve, s_pv, u - 1)
                    dve.tensor_copy(probs_t[0:TAIL, k % 2, (KT - 1) * P:KT * P],
                                    ps_turn[0:TAIL, (GROUPS - 1) % 2, 0:P]).then_inc(s_pt_dve, 1)
                if is_unit(u - 1):
                    ln2(i, k - 1)
                if is_unit(u - 4):
                    gates(i, k - 4)
                if k % 2 == 1 and is_unit(u + 3):
                    ln1(i + 1, k // 2)

            dve.wait_ge(s_mask, 16)
            dve.tensor_scalar(mbias_rows[:], mask_i[:], 0, MASKED, ALU.is_equal, ALU.mult).then_inc(s_mrows, 1)
            dve.wait_ge(s_iota, 1)
            ln1(0, 0)
            prep_gt(0, 0)
            maximum(0, 0)
            ln1(0, 1)
            dve.wait_ge(s_consts, N_CONSTS)
            def dispatch(g):
                us = slice(g * GU, (g + 1) * GU)
                done = [g * PLAN_STEPS]

                def then(instruction):
                    done[0] += 1
                    instruction.then_inc(s_plan, 1)
                    dve.wait_ge(s_plan, done[0])

                if g == 0:
                    dve.wait_ge(s_tables, 7)
                dve.wait_ge(s_gates, (g + 1) * GU)
                then(dve.tensor_tensor(chosen[:], hot[:, 0, us], hot[:, 1, us], ALU.add))
                dve.wait_ge(s_rank, g + 1)
                dve.tensor_copy(rank[:].rearrange("p u e -> p (u e)"), ps_misc[:, 0:GU * E])
                then(dve.tensor_copy(total[:], ps_misc[:, GU * E:2 * GU * E].rearrange("p (u e) -> p e u", e=E)))
                then(dve.tensor_tensor_scan(flat(upto), flat(keep), flat(total), 0.0, ALU.mult, ALU.add))
                then(dve.tensor_tensor(filled[:], upto[:, :, GU - 1:GU].broadcast_to([P, E, GU]),
                                       rows128[:].unsqueeze(1).broadcast_to([P, E, GU]), ALU.is_gt))
                then(dve.tensor_reduce(blocks[:], filled[:], AX.X, ALU.add))
                then(dve.tensor_tensor_scan(blocks_end[:], ones[:, 0:E], blocks[:], 0.0, ALU.mult, ALU.add))
                dve.tensor_tensor(past[:], blocks_end[:].unsqueeze(1).broadcast_to([P, GB, E]),
                                  count_f[:].unsqueeze(2).broadcast_to([P, GB, E]), ALU.is_le)
                then(dve.tensor_tensor(blocks[:], blocks_end[:], blocks[:], ALU.subtract))
                dve.tensor_reduce(owner_f[:], past[:], AX.X, ALU.add)
                then(dve.tensor_tensor(first[:], upto[:], total[:], ALU.subtract))
                then(dve.scalar_tensor_tensor(first[:], blocks[:].unsqueeze(2).broadcast_to([P, E, GU]), float(P), first[:],
                                              ALU.mult, ALU.add))
                dve.tensor_scalar(owner[:, g * GB:(g + 1) * GB], owner_f[:], E - 1.0, None, ALU.min).then_inc(s_owner, 1)
                then(dve.tensor_tensor(spot[:], rank[:], first[:].rearrange("p e u -> p u e"), ALU.add))
                for c in range(TOP_K):
                    last = dve.tensor_tensor(spot_k[:, c], hot[:, c, us], spot[:], ALU.mult)
                then(last)
                then(dve.tensor_reduce(place_f[:], spot_k[:], AX.X, ALU.add))
                dve.tensor_copy(place[:, :, us], place_f[:]).then_inc(s_place, 1)
                assert done[0] == (g + 1) * PLAN_STEPS

            def flat(t):
                return t[:].rearrange("p a b -> p (a b)")

            slots(dve, slot, lambda: dispatch(0))
            dispatch(1)

            def step(i, k):
                m = SB * i + k
                if is_block(m):
                    dve.wait_ge(s_th, m + 1)
                    dve.scalar_tensor_tensor(sg[:, k % 2], th[:, k % 2], 1.0, ps[:, 2 + k % 2, H:H2], ALU.add,
                                             ALU.mult).then_inc(s_sg, 1)
                    dve.wait_ge(s_sg, m + 1)
                    wait(dve, s_ht, m - 1)
                    dve.scalar_tensor_tensor(hid[:, k % 2], sg[:, k % 2], 0.5, ps[:, 2 + k % 2, 0:H], ALU.mult,
                                             ALU.mult).then_inc(s_h, 1)
                if is_block(m - 2):
                    i2, k2 = shift(i, k, -2, SB)
                    dve.wait_ge(s_down, m - 1)
                    if k2 % CH == 0:
                        wait(dve, s_ybuf[k2 // CH], 16 * i2)
                    dve.tensor_copy(blk_y[:, k2 // CH, k2 % CH], ps[:, 6 + k % 2, 0:D]).then_inc(s_y2, 1)

            steps(dve, step)

            for u in range(UNITS):
                g, n = u // GU, u % GU
                dve.wait_ge(s_got[n], 16 * TOP_K * (g + 1))
                dve.scalar_tensor_tensor(base_all[:, u], got[:, n, 0], gate_all[:, u, 0:1], base_all[:, u], ALU.mult,
                                         ALU.add).then_inc(s_part, 1)
                dve.wait_ge(s_part, u + 1)
                dve.scalar_tensor_tensor(base_all[:, u], got[:, n, 1], gate_all[:, u, 1:2], base_all[:, u], ALU.mult,
                                         ALU.add).then_inc(s_final, 1)

        @block.tensor
        def _(pe):
            pe.wait_ge(s_consts, N_CONSTS)
            pe.wait_ge(s_ident, 1)

            def prep_xt(i, j, routed):
                b = 2 * i + j
                pe.wait_ge(s_xn1, b + 1)
                wait(pe, s_lg, routed)
                wait(pe, s_qbk, b)
                for t in range(QT):
                    last = pe.transpose(ps_misc[:, t * P:(t + 1) * P], xn1[:, j, t], ident[:])
                last.then_inc(s_xt, 1)

            def prep_qt(i, j):
                b = 2 * i + j
                pe.wait_ge(s_xtc, b + 1)
                pe.matmul(ps_misc[:, 0:SQ], wq_sb[:], xt_sb[:], start=True, stop=True).then_inc(s_qt, 1)

            def prep_gt(i, j):
                b = 2 * i + j
                pe.wait_ge(s_qtc, b + 1)
                pe.matmul(ps_misc[:, 0:SQ], wkt_sb[:], qt_sb[:], start=True, stop=True)
                for t in range(QT):
                    last = pe.matmul(ps_misc[:, SQ + t:SQ + t + 1], qt_sb[:, t * P:(t + 1) * P], bk_col[:],
                                     start=True, stop=True)
                last.then_inc(s_gt, 1)

            def score(i, k):
                u = 4 * i + k
                j = k // 2
                pe.wait_ge(s_gtc, 2 * i + j + 1)
                pe.wait_ge(s_ctxt[j], 16 * (i + 1))
                wait(pe, s_max, u)
                for c in range(0, SK, BANK):
                    n = min(BANK, SK - c)
                    last = pe.matmul(ps_scores[:, c:c + n], gt_sb[:, j, (k % 2) * P:(k % 2 + 1) * P],
                                     ctxt_sb[:, j, c:c + n], start=True, stop=True)
                last.then_inc(s_scores, 1)

            def turn(i, k, g):
                u = 4 * i + k
                if g == 0:
                    pe.wait_ge(s_exp, u + 1)
                if g < 2:
                    wait(pe, *((s_pt_act, 3 * u) if g == 0 else (s_pt_dve, u)))
                else:
                    pe.wait_ge(s_pt_act, 3 * u + g - 1)
                for t in range(4 * g, min(4 * g + 4, KT)):
                    n = batch_part(t)
                    last = pe.transpose(ps_turn[0:n, g % 2, (t - 4 * g) * P:(t - 4 * g + 1) * P],
                                        probs[:, k % 2, t * P:t * P + n], ident[:])
                last.then_inc(s_turned, 1)

            def times_ctx(i, k, g):
                u = 4 * i + k
                j = k // 2
                if g == 0:
                    pe.wait_ge(s_ctx[j], 32 * (i + 1))
                    wait(pe, s_x1, u)
                if g < GROUPS - 1:
                    pe.wait_ge(s_pt_act, 3 * u + g + 1)
                else:
                    pe.wait_ge(s_pt_dve, u + 1)
                for t in range(4 * g, min(4 * g + 4, KT)):
                    n = batch_part(t)
                    last = pe.matmul(ps_o[:, 0:P], ctx_sb[0:n, j, t], probs_t[0:n, k % 2, t * P:(t + 1) * P],
                                     start=t == 0, stop=t == KT - 1)
                if g == GROUPS - 1:
                    last.then_inc(s_pv, 1)

            def slot(i, k):
                u = 4 * i + k
                nxt = (i, k // 2 + 1) if k < 2 else (i + 1, 0)
                prep = k % 2 == 0 and is_unit(u + 2)
                if is_unit(u + 1):
                    score(*((i, k + 1) if k < 3 else (i + 1, 0)))
                if is_unit(u - 1):
                    pe.wait_ge(s_ot, u)
                    pe.matmul(ps_o[:, 0:D], o_t[:, (k - 1) % 2], wv_sb[:], start=True, stop=True).then_inc(s_attn, 1)
                if is_unit(u - 3):
                    pe.wait_ge(s_rtc, u - 2)
                    pe.matmul(ps_misc[:, 0:E], xnt[:, (k - 3) % 2], wr_sb[:], start=True, stop=True).then_inc(s_logits, 1)
                if prep:
                    prep_xt(*nxt, u - 2)
                if is_unit(u):
                    turn(i, k, 0)
                    turn(i, k, 1)
                    times_ctx(i, k, 0)
                if prep:
                    prep_qt(*nxt)
                if is_unit(u):
                    turn(i, k, 2)
                    times_ctx(i, k, 1)
                if prep:
                    prep_gt(*nxt)
                if is_unit(u):
                    turn(i, k, 3)
                    times_ctx(i, k, 2)
                    times_ctx(i, k, 3)
                if is_unit(u - 2):
                    pe.wait_ge(s_xn2, u - 1)
                    wait(pe, s_lg, u - 2)
                    if prep:
                        pe.wait_ge(s_qbk, 2 * nxt[0] + nxt[1] + 1)
                    pe.transpose(ps_misc[:, 0:P], xn2[:, (k - 2) % 2], ident[:]).then_inc(s_rt, 1)

            prep_xt(0, 0, 0)
            prep_qt(0, 0)
            prep_gt(0, 0)
            score(0, 0)

            def rank_rows(g):
                pe.wait_ge(s_plan, g * PLAN_STEPS + 1)
                pe.wait_ge(s_lg, min((g + 1) * GU + 1, UNITS))
                pe.wait_ge(s_rtc, min((g + 1) * GU + 2, UNITS))
                rows = chosen[:].rearrange("p u e -> p (u e)")
                pe.matmul(ps_misc[:, 0:GU * E], before[:], rows, start=True, stop=True)
                pe.matmul(ps_misc[:, GU * E:2 * GU * E], ones[:], rows, start=True, stop=True).then_inc(s_rank, 1)
                pe.wait_ge(s_plan, g * PLAN_STEPS + 2)

            slots(pe, slot, lambda: rank_rows(0))
            rank_rows(1)

            def turn_block(i, k):
                m = SB * i + k
                if k % CH == 0:
                    pe.wait_ge(s_blk[k // CH], 16 * (i + 1))
                wait(pe, s_bxc, m - 1)
                pe.transpose(ps[:, k % 2, 0:P], blk_x[:, k // CH, k % CH], ident[:]).then_inc(s_bxt, 1)

            owner_regs = [pe.alloc_register(f"owner{k}") for k in range(SB)]

            def load_owner(i, k):
                pe.load([owner_regs[k]], owner[0:1, bass.ds(SB * i + k, 1)])

            def expert(k):
                return pe.snap(owner_regs[k], min_val=0, max_val=E - 1)

            def step(i, k):
                m = SB * i + k
                if is_block(m + 1):
                    turn_block(*shift(i, k, 1, SB))
                if is_block(m):
                    e = expert(k)
                    pe.wait_ge(s_bxc, m + 1)
                    wait(pe, s_h, m - 1)
                    pe.matmul(ps[:, 2 + k % 2], blk_xt[:, k % 2], wup_sb[:, bass.ds(e, 1)].rearrange("p a h -> p (a h)"),
                              start=True, stop=True).then_inc(s_up, 1)
                    if is_block(m + 1):
                        load_owner(*shift(i, k, 1, SB))
                if is_block(m - 1):
                    pe.wait_ge(s_h, m)
                    wait(pe, s_htc, m - 2)
                    for c in range(HC):
                        last = pe.transpose(ps[:, 4 + (k - 1) % 2, c * P:(c + 1) * P], hid[:, (k - 1) % 2, c * P:(c + 1) * P],
                                            ident[:])
                    last.then_inc(s_ht, 1)
                if is_block(m - 2):
                    e = expert((k - 2) % SB)
                    pe.wait_ge(s_htc, m - 1)
                    wait(pe, s_y2, m - 3)
                    for c in range(HC):
                        last = pe.matmul(ps[:, 6 + k % 2, 0:D], hid_t[:, k % 2, c * P:(c + 1) * P],
                                         wdn_sb[:, bass.ds(e, 1), c].rearrange("p a d -> p (a d)"),
                                         start=c == 0, stop=c == HC - 1)
                    last.then_inc(s_down, 1)

            pe.wait_ge(s_experts, 32)
            pe.wait_ge(s_max, UNITS)
            pe.wait_ge(s_pt_dve, UNITS)
            pe.wait_ge(s_pt_act, 3 * UNITS)
            pe.wait_ge(s_x1, UNITS)
            pe.wait_ge(s_owner, GROUPS_D)
            load_owner(0, 0)
            turn_block(0, 0)
            steps(pe, step)


def kernel(x, ctx_1024, mask_BxS2_ik0, L0_xattn_Wq, L0_xattn_bq, L0_xattn_Wk, L0_xattn_bk, L0_xattn_Wv,
           L0_xattn_bv, L0_ffn_norm_scale, L0_ffn_w_router, L0_ffn_w_up, L0_ffn_w_down):
    import numpy as np
    import concourse.bacc as bacc
    from concourse.bass_utils import run_bass_kernel_spmd

    def turned(a, *axes):
        return np.ascontiguousarray(np.asarray(a).transpose(*axes))

    arrays = {
        "x": np.ascontiguousarray(x),
        "ctx_rows": np.ascontiguousarray(ctx_1024),
        "ctx_cols": turned(ctx_1024, 0, 2, 1),
        "mask": np.ascontiguousarray(mask_BxS2_ik0),
        "wq": np.ascontiguousarray(L0_xattn_Wq),
        "wk_t": turned(L0_xattn_Wk, 1, 0),
        "wv": np.ascontiguousarray(L0_xattn_Wv),
        "bq": np.asarray(L0_xattn_bq).reshape(-1, 1),
        "bk": np.asarray(L0_xattn_bk).reshape(-1, 1),
        "bv": np.ascontiguousarray(L0_xattn_bv),
        "norm_scale": np.ascontiguousarray(L0_ffn_norm_scale),
        "w_router_t": turned(L0_ffn_w_router, 1, 0),
        "w_up_t": turned(L0_ffn_w_up, 0, 2, 1),
        "w_down_t": turned(L0_ffn_w_down, 0, 2, 1),
    }
    nc = bacc.Bacc("TRN2", target_bir_lowering=False, num_devices=1)
    aps = [nc.dram_tensor(n, a.shape, mybir.dt.from_np(a.dtype), kind="ExternalInput").ap() for n, a in arrays.items()]
    out = nc.dram_tensor("out", arrays["x"].shape, F32, kind="ExternalOutput").ap()
    xattn_moe(nc, *aps, out)
    result = run_bass_kernel_spmd(nc, [arrays], core_ids=[0])
    return result.results[0]["out"]
```

```python
from contextlib import ExitStack

import concourse.bass as bass
from concourse import mybir

F32 = mybir.dt.float32
I32 = mybir.dt.int32
U32 = mybir.dt.uint32
ALU = mybir.AluOpType
ACT = mybir.ActivationFunctionType
AX = mybir.AxisListType

P = 128
LN_EPS = 1e-5
RMS_EPS = 1e-6
MASKED = -1e30
LOWEST = -3.4e38
BANK = 512


def wait(eng, sem, value):
    if not isinstance(value, int) or value > 0:
        eng.wait_ge(sem, value)


def xattn_moe(nc, x, ctx_rows, ctx_cols, mask, wq, wk_t, wv, bq, bk, bv, norm_scale, w_router_t,
              w_up_t, w_down_t, out):
    B, SQ, D = x.shape
    SK = ctx_rows.shape[1]
    E, _, H2 = w_up_t.shape
    H = H2 // 2
    QT = SQ // P
    UNITS = B * QT
    TOK = B * SQ
    KT = -(-SK // P)
    TAIL = SK - (KT - 1) * P
    GROUPS = -(-KT // 4)
    HC = H // P
    SCALE = float(D) ** -0.5
    assert D == P and QT == 2 and B % 2 == 0 and B >= 6 and GROUPS == 4 and TAIL < P and HC == 2 and E == 8
    PAIRS = B // 2
    RING = 4
    TOP_K = 2
    GROUPS_D = 2
    GU = UNITS // GROUPS_D
    GB = TOP_K * GU + E
    NB = GROUPS_D * GB
    CH = 4
    SB = 2 * CH
    GC = GB // CH
    SPLIT = GU // 4 + 1
    assert GB % SB == 0 and GU % 4 == 0 and 1 < SPLIT < PAIRS - 1

    def batch_part(t):
        return P if t < KT - 1 else TAIL

    x_tiles = x.rearrange("b (t p) d -> b p t d", p=P)
    out_tiles = out.rearrange("b (t p) d -> p (b t) d", p=P)

    rows_in = [nc.dram_tensor(f"rows_in{g}", [GB * P, D], F32, kind="Internal").ap() for g in range(GROUPS_D)]
    rows_out = [nc.dram_tensor(f"rows_out{g}", [GB * P, D], F32, kind="Internal").ap() for g in range(GROUPS_D)]
    mbias_dram = nc.dram_tensor("mbias_dram", [B, SK], F32, kind="Internal").ap()

    st = ExitStack()
    with st:
        def sb(name, shape, dt=F32):
            return st.enter_context(nc.sbuf_tensor(name, shape, dt))

        def sem(name):
            return st.enter_context(nc.semaphore(name))

        wq_sb = sb("wq_sb", [P, D])
        wkt_sb = sb("wkt_sb", [P, D])
        wv_sb = sb("wv_sb", [P, D])
        wr_sb = sb("wr_sb", [P, E])
        wup_sb = sb("wup_sb", [P, E, H2])
        wdn_sb = sb("wdn_sb", [P, E, HC, D])
        bq_col = sb("bq_col", [P, 1])
        bk_col = sb("bk_col", [P, 1])
        bv_rows = sb("bv_rows", [P, D])
        norm_rows = sb("norm_rows", [P, D])
        ident = sb("ident", [P, P])
        spare = sb("spare", [P, 8])
        minus_half = sb("minus_half", [P, QT])
        iota_i = sb("iota_i", [P, E], I32)
        iota_f = sb("iota_f", [P, E])
        x_in = sb("x_in", [P, 2, QT, D])
        xn1 = sb("xn1", [P, 2, QT, D])
        ctx_sb = sb("ctx_sb", [P, 2, KT, D])
        ctxt_sb = sb("ctxt_sb", [P, 2, SK])
        mask_i = sb("mask_i", [B, SK], I32)
        mbias_rows = sb("mbias_rows", [B, SK])
        mbias = sb("mbias", [P, 2, SK])
        xt_sb = sb("xt_sb", [P, SQ])
        qt_sb = sb("qt_sb", [P, SQ])
        gt_sb = sb("gt_sb", [P, 2, SQ])
        qbk = sb("qbk", [P, 2, QT])
        st1 = sb("st1", [P, QT, 6])
        mv1 = sb("mv1", [P, QT, 2])
        ve1 = sb("ve1", [P, QT])
        rstd1 = sb("rstd1", [P, QT])
        scores = sb("scores", [P, 2, SK])
        probs = sb("probs", [P, 2, SK])
        probs_t = sb("probs_t", [P, 2, KT * P])
        smax = sb("smax", [P, RING])
        smax2 = sb("smax2", [P, RING])
        ebias = sb("ebias", [P, RING])
        esum = sb("esum", [P, RING])
        rsum = sb("rsum", [P, RING])
        o_t = sb("o_t", [P, 2, P])
        x1 = sb("x1", [P, RING, D])
        st2 = sb("st2", [P, 6])
        mv2 = sb("mv2", [P, 2])
        ve2 = sb("ve2", [P, 1])
        ms = sb("ms", [P, 1])
        rstd2 = sb("rstd2", [P, 1])
        y = sb("y", [P, 2, D])
        ysq = sb("ysq", [P, D])
        ss = sb("ss", [P, 1])
        rrms = sb("rrms", [P, 1])
        xn2 = sb("xn2", [P, 2, D])
        xnt = sb("xnt", [P, 2, P])
        logits = sb("logits", [P, E])
        top = sb("top", [P, 8])
        top_i = sb("top_i", [P, 8], U32)
        top_f = sb("top_f", [P, 2, 2])
        sdiff = sb("sdiff", [P, 1])
        e2 = sb("e2", [P, 2, 1])
        den = sb("den", [P, 1])
        hot = sb("hot", [P, TOP_K, UNITS, E])
        gate_all = sb("gate_all", [P, UNITS, TOP_K])
        xn2_all = sb("xn2_all", [P, UNITS, D])
        base_all = sb("base_all", [P, UNITS, D])
        place = sb("place", [P, TOP_K, UNITS], I32)
        ones = sb("ones", [P, P])
        before = sb("before", [P, P])
        zeros = sb("zeros", [P, D])
        keep = sb("keep", [P, E, GU])
        count_i = sb("count_i", [P, GB], I32)
        count_f = sb("count_f", [P, GB])
        rows128 = sb("rows128", [P, GU])
        rank = sb("rank", [P, GU, E])
        total = sb("total", [P, E, GU])
        upto = sb("upto", [P, E, GU])
        filled = sb("filled", [P, E, GU])
        blocks = sb("blocks", [P, E])
        blocks_end = sb("blocks_end", [P, E])
        first = sb("first", [P, E, GU])
        spot = sb("spot", [P, GU, E])
        spot_k = sb("spot_k", [P, TOP_K, GU, E])
        place_f = sb("place_f", [P, TOP_K, GU])
        past = sb("past", [P, GB, E])
        owner_f = sb("owner_f", [P, GB])
        owner = sb("owner", [P, NB], I32)
        blk_x = sb("blk_x", [P, 2, CH, D])
        blk_xt = sb("blk_xt", [P, 2, P])
        th = sb("th", [P, 2, H])
        sg = sb("sg", [P, 2, H])
        hid = sb("hid", [P, 2, H])
        hid_t = sb("hid_t", [P, 2, HC * P])
        blk_y = sb("blk_y", [P, 2, CH, D])
        got = sb("got", [P, GU, TOP_K, D])

        ps = st.enter_context(nc.psum_tensor("ps", [P, 8, BANK], F32))
        ps_scores = ps[:, 0:4, :].rearrange("p a b -> p (a b)")
        ps_turn = ps[:, 4:6, :]
        ps_o = ps[:, 6, :]
        ps_misc = ps[:, 7, :]

        s_consts = sem("consts_loaded")
        s_experts = sem("experts_loaded")
        s_mbias = [sem(f"mbias_loaded{j}") for j in range(2)]
        s_x = [sem(f"x_loaded{j}") for j in range(2)]
        s_ctx = [sem(f"ctx_loaded{j}") for j in range(2)]
        s_ctxt = [sem(f"ctxt_loaded{j}") for j in range(2)]
        s_mask = sem("mask_loaded")
        s_mrows = sem("mask_bias_made")
        s_mstore = sem("mask_bias_stored")
        s_stored = sem("stored")
        s_cleared = sem("rows_cleared")
        s_blk = [sem(f"block_rows_loaded{j}") for j in range(2)]
        s_ybuf = [sem(f"result_buffer_stored{j}") for j in range(2)]
        s_scat = [sem(f"rows_scattered{g}") for g in range(GROUPS_D)]
        s_got = [sem(f"rows_gathered{n}") for n in range(GU)]
        s_pool = sem("pool_consts_set")
        s_ident = sem("ident_ready")
        s_xb = sem("x_plus_bv_ready")
        s_base = sem("base_ready")
        s_keep = sem("xn2_kept")
        s_zeros = sem("zeros_set")
        s_tables = sem("dispatch_tables_set")
        s_scores = sem("scores_ready")
        s_turned = sem("probs_turned")
        s_pv = sem("pv_done")
        s_attn = sem("attn_ready")
        s_xt = sem("xt_ready")
        s_qt = sem("qt_ready")
        s_gt = sem("gt_ready")
        s_rt = sem("rt_ready")
        s_logits = sem("logits_ready")
        s_rank = sem("rank_ready")
        s_bxt = sem("block_turned")
        s_up = sem("up_ready")
        s_ht = sem("hidden_turned")
        s_down = sem("down_ready")
        s_exp = sem("exp_done")
        s_pt_act = sem("probs_t_by_act")
        s_ot = sem("o_t_ready")
        s_xtc = sem("xt_copied")
        s_qtc = sem("qt_copied")
        s_rtc = sem("rt_copied")
        s_e2 = sem("e2_ready")
        s_bxc = sem("block_turned_copied")
        s_htc = sem("hidden_turned_copied")
        s_th = sem("tanh_ready")
        s_iota = sem("iota_ready")
        s_max = sem("max_done")
        s_max2 = sem("max2_done")
        s_ebias = sem("ebias_ready")
        s_gtc = sem("gt_copied")
        s_qbk = sem("qbk_copied")
        s_pt_dve = sem("probs_t_by_dve")
        s_rsum = sem("rsum_ready")
        s_x1 = sem("x1_ready")
        s_st1 = sem("ln1_stats")
        s_mv1 = sem("ln1_moments")
        s_ve1 = sem("ln1_var_eps")
        s_rs1 = sem("ln1_rstd")
        s_xn1 = sem("xn1_ready")
        s_st2 = sem("ln2_stats")
        s_mv2 = sem("ln2_moments")
        s_ve2 = sem("ln2_var_eps")
        s_ms = sem("mean_square_ready")
        s_rs2 = sem("ln2_rstd")
        s_y = sem("y_ready")
        s_ss = sem("ss_ready")
        s_rr = sem("rrms_ready")
        s_xn2 = sem("xn2_ready")
        s_lg = sem("logits_copied")
        s_top = sem("top_ready")
        s_topi = sem("top_index_ready")
        s_sd = sem("sdiff_ready")
        s_topf = sem("top_f_ready")
        s_den = sem("den_ready")
        s_w1 = sem("gate1_ready")
        s_w2 = sem("gate2_ready")
        s_hot = sem("hot_ready")
        s_gates = sem("gates_ready")
        s_sg = sem("sg_ready")
        s_h = sem("h_ready")
        s_y2 = sem("block_result_ready")
        s_plan = sem("dispatch_step")
        s_rankc = sem("rank_copied")
        s_place = sem("places_ready")
        PLAN_STEPS = 11
        s_owner = sem("owners_ready")
        s_part = sem("first_choice_added")
        s_final = sem("result_ready")

        block = st.enter_context(nc.Block())

        def is_unit(u):
            return not isinstance(u, int) or 0 <= u < UNITS

        def slots(eng, slot, between):
            for k in range(4):
                slot(0, k)
            with eng.Fori(1, SPLIT) as i:
                for k in range(4):
                    slot(i, k)
            between()
            with eng.Fori(SPLIT, PAIRS - 1) as i:
                for k in range(4):
                    slot(i, k)
            for k in range(4):
                slot(PAIRS - 1, k)
            for k in range(4):
                slot(PAIRS, k)

        def is_block(m):
            return not isinstance(m, int) or 0 <= m < NB

        def steps(eng, step):
            for k in range(SB):
                step(0, k)
            with eng.Fori(1, NB // SB - 1) as i:
                for k in range(SB):
                    step(i, k)
            for k in range(SB):
                step(NB // SB - 1, k)
            for k in range(2):
                step(NB // SB, k)

        def shift(i, k, d, n):
            return (i, k + d) if 0 <= k + d < n else (i + (1 if d > 0 else -1), k + d - (n if d > 0 else -n))

        @block.sync
        def _(sp):
            def load(i, j, first=False):
                b = 2 * i + j
                wait(sp, s_xn1, b - 1)
                wait(sp, s_xb, b - 1)
                sp.dma_start(x_in[:, j], x_tiles[b]).then_inc(s_x[j], 16)
                wait(sp, s_scores, QT * (b - 1))
                sp.dma_start(ctxt_sb[:, j], ctx_cols[b]).then_inc(s_ctxt[j], 16)
                if isinstance(i, int) and b == 0:
                    sp.wait_ge(s_mstore, 16)
                wait(sp, s_max, QT * (b - 1))
                sp.dma_start(mbias[:, j], mbias_dram[b].partition_broadcast(P)).then_inc(s_mbias[j], 16)
                wait(sp, s_pv, QT * (b - 1))
                sp.dma_start(ctx_sb[:, j, 0:KT - 1],
                             ctx_rows[b][0:(KT - 1) * P].rearrange("(t p) d -> p t d", p=P)).then_inc(s_ctx[j], 16)
                sp.dma_start(ctx_sb[0:TAIL, j, KT - 1], ctx_rows[b][(KT - 1) * P:SK]).then_inc(s_ctx[j], 16)

            sp.dma_start(mask_i[:], mask).then_inc(s_mask, 16)
            for dst, src in ((wq_sb[:], wq), (wkt_sb[:], wk_t), (bq_col[:], bq), (bk_col[:], bk)):
                sp.dma_start(dst, src).then_inc(s_consts, 16)
            load(0, 0)
            for dst, src in ((wv_sb[:], wv), (wr_sb[:], w_router_t), (bv_rows[:], bv.partition_broadcast(P)),
                             (norm_rows[:], norm_scale.partition_broadcast(P))):
                sp.dma_start(dst, src).then_inc(s_consts, 16)
            load(0, 1)
            sp.dma_start(wup_sb[:], w_up_t.rearrange("e d h -> d e h")).then_inc(s_experts, 16)
            sp.dma_start(wdn_sb[:], w_down_t.rearrange("e (c p) d -> p e c d", p=P)).then_inc(s_experts, 16)
            sp.wait_ge(s_zeros, 1)
            for g in range(GROUPS_D):
                sp.dma_start(rows_in[g].rearrange("(n p) d -> p n d", p=P),
                             zeros[:].unsqueeze(1).broadcast_to([P, GB, D])).then_inc(s_cleared, 16)
            with sp.Fori(1, PAIRS) as i:
                load(i, 0)
                load(i, 1)

            in_chunks = [t.rearrange("(c t p) d -> c p t d", t=CH, p=P) for t in rows_in]
            out_chunks = [t.rearrange("(c t p) d -> c p t d", t=CH, p=P) for t in rows_out]
            GI = GC // 2

            def load_chunk(g, i2, j):
                wait(sp, s_bxt, CH * (g * GC + 2 * i2 + j - 1))
                sp.dma_start(blk_x[:, j], in_chunks[g][2 * i2 + j]).then_inc(s_blk[j], 16)

            def store_chunk(g, i2, j):
                sp.wait_ge(s_y2, CH * (g * GC + 2 * i2 + j + 1))
                sp.dma_start(out_chunks[g][2 * i2 + j], blk_y[:, j]).then_inc(s_ybuf[j], 16)

            for g in range(GROUPS_D):
                sp.wait_ge(s_scat[g], 16 * TOP_K * GU)
                for j in range(2):
                    load_chunk(g, 0, j)
                    if g:
                        store_chunk(g - 1, GI - 1, j)
                with sp.Fori(0, GI - 1) as i2:
                    for j in range(2):
                        load_chunk(g, i2 + 1, j)
                        store_chunk(g, i2, j)
            for j in range(2):
                store_chunk(GROUPS_D - 1, GI - 1, j)

            for u in range(0, UNITS, 4):
                sp.wait_ge(s_final, u + 4)
                sp.dma_start(out_tiles[:, u:u + 4], base_all[:, u:u + 4]).then_inc(s_stored, 16)
            sp.wait_ge(s_stored, 16 * UNITS // 4)

        N_CONSTS = 8 * 16

        @block.gpsimd
        def _(pool):
            def make_xb(i, j):
                b = 2 * i + j
                pool.wait_ge(s_x[j], 16 * (i + 1))
                wait(pool, s_base, QT * (b - 1))
                wait(pool, s_xn2, QT * (b - 1))
                for t in range(QT):
                    last = pool.tensor_tensor(x1[:, 2 * j + t], x_in[:, j, t], bv_rows[:], ALU.add)
                last.then_inc(s_xb, 1)

            def rstd_of_x(i, j):
                pool.wait_ge(s_ve1, 2 * i + j + 1)
                wait(pool, s_xn1, 2 * i + j)
                pool.tensor_tensor(rstd1[:], ve1[:], minus_half[:], ALU.pow).then_inc(s_rs1, 1)

            def slot_first(i, k):
                u = 4 * i + k
                if is_unit(u - 2):
                    pool.wait_ge(s_y, u - 1)
                    pool.tensor_tensor(base_all[:, bass.ds(u - 2, 1)],
                                       x1[:, (k - 2) % 4:(k - 2) % 4 + 1], y[:, (k - 2) % 2:(k - 2) % 2 + 1],
                                       ALU.add).then_inc(s_base, 1)
                    pool.wait_ge(s_xn2, u - 1)
                    pool.tensor_copy(xn2_all[:, bass.ds(u - 2, 1)], xn2[:, (k - 2) % 2:(k - 2) % 2 + 1]).then_inc(s_keep, 1)
                if k % 2 == 1 and is_unit(u + 3):
                    rstd_of_x(i + 1, k // 2)
                if k == 3 and is_unit(u + 1):
                    make_xb(i + 1, 0)
                if k == 1 and is_unit(u):
                    make_xb(i, 1)

            def slot_second(i, k):
                u = 4 * i + k
                if is_unit(u - 1):
                    pool.wait_ge(s_ve2, u)
                    wait(pool, s_y, u - 1)
                    pool.tensor_tensor(rstd2[:], ve2[:], minus_half[:, 0:1], ALU.pow).then_inc(s_rs2, 1)
                    pool.wait_ge(s_ms, u)
                    wait(pool, s_xn2, u - 1)
                    pool.tensor_tensor(rrms[:], ms[:], minus_half[:, 0:1], ALU.pow).then_inc(s_rr, 1)

            def scatter(g, n):
                u, c = g * GU + n // TOP_K, n % TOP_K
                if n == 0:
                    pool.wait_ge(s_cleared, 16 * GROUPS_D)
                    pool.wait_ge(s_place, g + 1)
                    pool.wait_ge(s_keep, GU * (g + 1))
                pool.indirect_dma_start(rows_in[g], bass.IndirectOffsetOnAxis(ap=place[:, c, u:u + 1], axis=0),
                                        xn2_all[:, u], None).then_inc(s_scat[g], 16)

            pool.memset(zeros[:], 0.0).then_inc(s_zeros, 1)
            pool.memset(ident[:], 0.0).then_inc(s_pool, 1)
            pool.memset(minus_half[:], -0.5).then_inc(s_pool, 1)
            pool.iota(iota_i[:], pattern=[[1, E]], base=0, channel_multiplier=0).then_inc(s_pool, 1)
            pool.wait_ge(s_pool, 3)
            pool.affine_select(out=ident[:], in_=ident[:], compare_op=ALU.not_equal, fill=1.0, base=0,
                               pattern=[[-1, P]], channel_multiplier=1).then_inc(s_ident, 1)
            pool.tensor_copy(iota_f[:], iota_i[:]).then_inc(s_iota, 1)
            rstd_of_x(0, 0)
            rstd_of_x(0, 1)
            pool.memset(ones[:], 1.0).then_inc(s_tables, 1)
            pool.memset(keep[:], 1.0).then_inc(s_tables, 1)
            pool.iota(count_i[:], pattern=[[1, GB]], base=0, channel_multiplier=0).then_inc(s_tables, 1)
            pool.wait_ge(s_tables, 3)
            pool.memset(keep[:, :, 0:1], 0.0).then_inc(s_tables, 1)
            pool.affine_select(out=before[:], in_=ones[:], compare_op=ALU.is_gt, fill=0.0, base=0,
                               pattern=[[1, P]], channel_multiplier=-1).then_inc(s_tables, 1)
            pool.tensor_copy(count_f[:], count_i[:]).then_inc(s_tables, 1)
            pool.wait_ge(s_tables, 6)
            pool.tensor_scalar(rows128[:], count_f[:, 0:GU], float(P), None, ALU.mult).then_inc(s_tables, 1)
            pool.wait_ge(s_consts, N_CONSTS)
            make_xb(0, 0)

            for k in range(4):
                slot_first(0, k)
                slot_second(0, k)
            with pool.Fori(1, SPLIT) as i:
                for k in range(4):
                    slot_first(i, k)
                    slot_second(i, k)
            sent = 0
            for i in range(SPLIT, PAIRS + 1):
                for k in range(4):
                    slot_first(i, k)
                    for _ in range(min(3, TOP_K * GU - sent) if 4 * i + k > 4 * SPLIT else 0):
                        scatter(0, sent)
                        sent += 1
                    slot_second(i, k)
            for n in range(TOP_K * GU):
                scatter(1, n)
            for u in range(UNITS):
                g, n = u // GU, u % GU
                if n == 0:
                    for j in range(2):
                        pool.wait_ge(s_ybuf[j], 16 * (g + 1) * GC // 2)
                if g:
                    pool.wait_ge(s_final, u - GU + 1)
                for c in range(TOP_K):
                    pool.indirect_dma_start(got[:, n, c], None, rows_out[g],
                                            bass.IndirectOffsetOnAxis(ap=place[:, c, u:u + 1], axis=0)).then_inc(s_got[n], 16)

        @block.scalar
        def _(act):
            act.wait_ge(s_mrows, 1)
            act.dma_start(mbias_dram, mbias_rows[:]).then_inc(s_mstore, 16)
            act.wait_ge(s_consts, N_CONSTS)

            def prep_xt(i, j):
                b = 2 * i + j
                act.wait_ge(s_xt, b + 1)
                wait(act, s_qt, b)
                act.activation(xt_sb[:], ps_misc[:, 0:SQ], ACT.Copy).then_inc(s_xtc, 1)

            def prep_qt(i, j):
                b = 2 * i + j
                act.wait_ge(s_qt, b + 1)
                wait(act, s_gt, b)
                act.activation(qt_sb[:], ps_misc[:, 0:SQ], ACT.Identity, bias=bq_col[:]).then_inc(s_qtc, 1)

            def exp_unit(i, k):
                u = 4 * i + k
                act.wait_ge(s_ebias, u + 1)
                wait(act, s_turned, GROUPS * (u - 1))
                wait(act, s_rsum, u - 3)
                act.activation(probs[:, k % 2], scores[:, k % 2], ACT.Exp, bias=ebias[:, k:k + 1], scale=SCALE,
                               accum_out=esum[:, k:k + 1]).then_inc(s_exp, 1)

            def slot(i, k):
                u = 4 * i + k
                nxt = (i, k // 2 + 1) if k < 2 else (i + 1, 0)
                prep = k % 2 == 0 and is_unit(u + 2)
                if prep:
                    prep_xt(*nxt)
                if is_unit(u):
                    wait(act, s_pv, u - 1)
                    for g in range(GROUPS - 1):
                        if g == 2 and prep:
                            prep_qt(*nxt)
                        act.wait_ge(s_turned, GROUPS * u + g + 1)
                        act.activation(probs_t[:, k % 2, g * BANK:(g + 1) * BANK], ps_turn[:, g % 2],
                                       ACT.Copy).then_inc(s_pt_act, 1)
                if is_unit(u + 1):
                    exp_unit(*((i, k + 1) if k < 3 else (i + 1, 0)))
                if is_unit(u):
                    act.wait_ge(s_pv, u + 1)
                    wait(act, s_attn, u - 1)
                    act.activation(o_t[:, k % 2], ps_o[:, 0:P], ACT.Copy).then_inc(s_ot, 1)
                if is_unit(u - 3):
                    act.wait_ge(s_sd, u - 2)
                    wait(act, s_gates, u - 4)
                    act.activation(e2[:, (k - 3) % 2], sdiff[:], ACT.Exp).then_inc(s_e2, 1)
                if is_unit(u - 2):
                    act.wait_ge(s_rt, u - 1)
                    wait(act, s_logits, u - 3)
                    act.activation(xnt[:, k % 2], ps_misc[:, 0:P], ACT.Copy).then_inc(s_rtc, 1)

            prep_xt(0, 0)
            prep_qt(0, 0)
            exp_unit(0, 0)
            slots(act, slot, lambda: None)

            def block_xt(i, k):
                m = SB * i + k
                act.wait_ge(s_bxt, m + 1)
                wait(act, s_up, m - 1)
                act.activation(blk_xt[:, k % 2], ps[:, k % 2, 0:P], ACT.Copy).then_inc(s_bxc, 1)

            def step(i, k):
                m = SB * i + k
                if is_block(m + 1):
                    block_xt(*shift(i, k, 1, SB))
                if is_block(m):
                    act.wait_ge(s_up, m + 1)
                    wait(act, s_sg, m - 1)
                    act.activation(th[:, k % 2], ps[:, 2 + k % 2, H:H2], ACT.Tanh, scale=0.5).then_inc(s_th, 1)
                if is_block(m - 1):
                    act.wait_ge(s_ht, m)
                    wait(act, s_down, m - 2)
                    act.activation(hid_t[:, (k - 1) % 2], ps[:, 4 + (k - 1) % 2, 0:HC * P], ACT.Copy).then_inc(s_htc, 1)

            block_xt(0, 0)
            steps(act, step)

        @block.vector
        def _(dve):
            def take_waits(n):
                dve.memset(spare[:, n:n + 1], 0.0)


            def ln1_stats(i, j):
                dve.wait_ge(s_x[j], 16 * (i + 1))
                for t in range(QT):
                    last = dve.bn_stats(st1[:, t], x_in[:, j, t])
                last.then_inc(s_st1, 1)

            def ln1_moments(i, j):
                dve.wait_ge(s_st1, 2 * i + j + 1)
                take_waits(0)
                for t in range(QT):
                    last = dve.bn_aggr(mv1[:, t], st1[:, t])
                last.then_inc(s_mv1, 1)

            def ln1_var(i, j):
                dve.wait_ge(s_mv1, 2 * i + j + 1)
                dve.tensor_scalar(ve1[:], mv1[:, :, 1], LN_EPS, None, ALU.add).then_inc(s_ve1, 1)

            def ln1_norm(i, j):
                b = 2 * i + j
                dve.wait_ge(s_rs1, b + 1)
                wait(dve, s_xt, b - 1)
                for t in range(QT):
                    last = dve.tensor_scalar(xn1[:, j, t], x_in[:, j, t], mv1[:, t, 0:1], rstd1[:, t:t + 1],
                                             ALU.subtract, ALU.mult)
                last.then_inc(s_xn1, 1)

            def prep_gt(i, j):
                b = 2 * i + j
                dve.wait_ge(s_gt, b + 1)
                wait(dve, s_scores, QT * (b - 1))
                dve.tensor_copy(gt_sb[:, j], ps_misc[:, 0:SQ]).then_inc(s_gtc, 1)
                wait(dve, s_ebias, QT * (b - 1))
                dve.tensor_copy(qbk[:, j], ps_misc[:, SQ:SQ + QT]).then_inc(s_qbk, 1)

            def maximum(i, k):
                u = 4 * i + k
                j = k // 2
                dve.wait_ge(s_scores, u + 1)
                dve.wait_ge(s_mbias[j], 16 * (i + 1))
                wait(dve, s_exp, u - 1)
                take_waits(1)
                dve.tensor_tensor_reduce(out=scores[:, k % 2], in0=ps_scores[:, 0:SK], in1=mbias[:, j], scale=1.0,
                                         scalar=LOWEST, op0=ALU.add, op1=ALU.max,
                                         accum_out=smax[:, k:k + 1]).then_inc(s_max, 1)

            def bias_sum(i, k):
                u = 4 * i + k
                j = k // 2
                dve.wait_ge(s_max, u + 1)
                dve.wait_ge(s_qbk, 2 * i + j + 1)
                dve.tensor_scalar(smax2[:, k:k + 1], smax[:, k:k + 1], qbk[:, j, k % 2:k % 2 + 1], -SCALE, ALU.add,
                                  ALU.mult).then_inc(s_max2, 1)

            def bias(i, k):
                u = 4 * i + k
                dve.wait_ge(s_max2, u + 1)
                dve.scalar_tensor_tensor(ebias[:, k:k + 1], qbk[:, k // 2, k % 2:k % 2 + 1], SCALE, smax2[:, k:k + 1],
                                         ALU.mult, ALU.add).then_inc(s_ebias, 1)

            def post_sum(i, kk):
                u = 4 * i + kk
                r = kk % RING
                dve.wait_ge(s_exp, u + 1)
                dve.reciprocal(rsum[:, r:r + 1], esum[:, r:r + 1]).then_inc(s_rsum, 1)

            def post(i, kk):
                u = 4 * i + kk
                r = kk % RING
                dve.wait_ge(s_rsum, u + 1)
                dve.wait_ge(s_attn, u + 1)
                dve.wait_ge(s_xb, (2 * i + kk // 2 + 1))
                dve.scalar_tensor_tensor(x1[:, r], ps_o[:, 0:D], rsum[:, r:r + 1], x1[:, r], ALU.mult,
                                         ALU.add).then_inc(s_x1, 1)

            def ln2_stats(i, kk):
                u = 4 * i + kk
                dve.wait_ge(s_x1, u + 1)
                dve.bn_stats(st2[:], x1[:, kk % RING]).then_inc(s_st2, 1)

            def ln2_moments(i, kk):
                dve.wait_ge(s_st2, 4 * i + kk + 1)
                take_waits(2)
                dve.bn_aggr(mv2[:], st2[:]).then_inc(s_mv2, 1)

            def ln2_var(i, kk):
                dve.wait_ge(s_mv2, 4 * i + kk + 1)
                dve.tensor_scalar(ve2[:], mv2[:, 1:2], LN_EPS, None, ALU.add).then_inc(s_ve2, 1)

            def ln2_norm(i, kk):
                u = 4 * i + kk
                dve.wait_ge(s_rs2, u + 1)
                wait(dve, s_base, u - 1)
                dve.tensor_scalar(y[:, kk % 2], x1[:, kk % RING], mv2[:, 0:1], rstd2[:], ALU.subtract,
                                  ALU.mult).then_inc(s_y, 1)

            def rms_sum(i, kk):
                u = 4 * i + kk
                dve.wait_ge(s_y, u + 1)
                dve.tensor_tensor_reduce(out=ysq[:], in0=y[:, kk % 2], in1=y[:, kk % 2], scale=1.0, scalar=0.0,
                                         op0=ALU.mult, op1=ALU.add, accum_out=ss[:]).then_inc(s_ss, 1)

            def rms_mean(i, kk):
                dve.wait_ge(s_ss, 4 * i + kk + 1)
                dve.tensor_scalar(ms[:], ss[:], 1.0 / D, RMS_EPS, ALU.mult, ALU.add).then_inc(s_ms, 1)

            def rms_norm(i, kk):
                u = 4 * i + kk
                dve.wait_ge(s_rr, u + 1)
                wait(dve, s_rt, u - 1)
                wait(dve, s_keep, u - 1)
                dve.scalar_tensor_tensor(xn2[:, kk % 2], y[:, kk % 2], rrms[:], norm_rows[:], ALU.mult,
                                         ALU.mult).then_inc(s_xn2, 1)

            def take_logits(i, kk):
                u = 4 * i + kk
                dve.wait_ge(s_logits, u + 1)
                dve.tensor_copy(logits[:], ps_misc[:, 0:E]).then_inc(s_lg, 1)

            def best(i, kk):
                dve.wait_ge(s_lg, 4 * i + kk + 1)
                take_waits(3)
                dve.max(top[:], logits[:]).then_inc(s_top, 1)

            def best_index(i, kk):
                dve.wait_ge(s_top, 4 * i + kk + 1)
                take_waits(4)
                dve.max_index(top_i[:], top[:], logits[:]).then_inc(s_topi, 1)

            def best_difference(i, kk):
                wait(dve, s_e2, 4 * i + kk)
                dve.tensor_tensor(sdiff[:], top[:, 1:2], top[:, 0:1], ALU.subtract).then_inc(s_sd, 1)

            def best_number(i, kk):
                dve.wait_ge(s_topi, 4 * i + kk + 1)
                dve.tensor_copy(top_f[:, kk % 2], top_i[:, 0:2]).then_inc(s_topf, 1)

            def unit_gates(i, kk):
                return gate_all[:, bass.ds(4 * i + kk, 1)].rearrange("p a c -> p (a c)")

            def gates_sum(i, kk):
                dve.wait_ge(s_e2, 4 * i + kk + 1)
                dve.tensor_scalar(den[:], e2[:, kk % 2], 1.0, None, ALU.add).then_inc(s_den, 1)

            def gates_hot(i, kk):
                u = 4 * i + kk
                dve.wait_ge(s_topf, u + 1)
                for c in range(TOP_K):
                    dve.tensor_scalar(hot[:, c, bass.ds(u, 1)].rearrange("p a e -> p (a e)"), iota_f[:],
                                      top_f[:, kk % 2, c:c + 1], None, ALU.is_equal)

            def gates_first(i, kk):
                dve.wait_ge(s_den, 4 * i + kk + 1)
                dve.reciprocal(unit_gates(i, kk)[:, 0:1], den[:]).then_inc(s_w1, 1)

            def gates_second(i, kk):
                dve.wait_ge(s_w1, 4 * i + kk + 1)
                w = unit_gates(i, kk)
                dve.tensor_tensor(w[:, 1:2], w[:, 0:1], e2[:, kk % 2], ALU.mult).then_inc(s_gates, 1)

            def last_probs_t(i, k):
                u = 4 * i + k
                dve.wait_ge(s_turned, GROUPS * (u + 1))
                wait(dve, s_pv, u - 1)
                dve.tensor_copy(probs_t[0:TAIL, k % 2, (KT - 1) * P:KT * P],
                                ps_turn[0:TAIL, (GROUPS - 1) % 2, 0:P]).then_inc(s_pt_dve, 1)

            def slot(i, k):
                u = 4 * i + k
                nxt = (i, k // 2 + 1) if k < 2 else (i + 1, 0)
                following = (i, k + 1) if k < 3 else (i + 1, 0)
                prep = k % 2 == 0 and is_unit(u + 2)
                ln1 = k % 2 == 1 and is_unit(u + 3)
                ahead = (i + 1, k // 2)
                if is_unit(u - 4):
                    gates_sum(i, k - 4)
                if ln1:
                    ln1_stats(*ahead)
                if is_unit(u - 4):
                    gates_hot(i, k - 4)
                    gates_first(i, k - 4)
                if is_unit(u - 2):
                    rms_norm(i, k - 2)
                if is_unit(u - 4):
                    gates_second(i, k - 4)
                if ln1:
                    ln1_moments(*ahead)
                if is_unit(u - 1):
                    post_sum(i, k - 1)
                if ln1:
                    ln1_var(*ahead)
                if is_unit(u - 1):
                    post(i, k - 1)
                if is_unit(u - 3):
                    take_logits(i, k - 3)
                if is_unit(u + 1):
                    maximum(*following)
                if is_unit(u - 3):
                    best(i, k - 3)
                if is_unit(u + 1):
                    bias_sum(*following)
                if is_unit(u - 3):
                    best_index(i, k - 3)
                if is_unit(u + 1):
                    bias(*following)
                if is_unit(u - 3):
                    best_difference(i, k - 3)
                if is_unit(u - 1):
                    ln2_stats(i, k - 1)
                if is_unit(u - 3):
                    best_number(i, k - 3)
                if is_unit(u - 1):
                    ln2_moments(i, k - 1)
                if ln1:
                    ln1_norm(*ahead)
                if is_unit(u - 1):
                    ln2_var(i, k - 1)
                if is_unit(u) and not prep:
                    last_probs_t(i, k)
                if is_unit(u - 1):
                    ln2_norm(i, k - 1)
                if prep:
                    prep_gt(*nxt)
                if is_unit(u) and prep:
                    last_probs_t(i, k)
                if is_unit(u - 1):
                    rms_sum(i, k - 1)
                    rms_mean(i, k - 1)

            dve.wait_ge(s_mask, 16)
            dve.tensor_scalar(mbias_rows[:], mask_i[:], 0, MASKED, ALU.is_equal, ALU.mult).then_inc(s_mrows, 1)
            dve.wait_ge(s_iota, 1)
            def ln1(i, j):
                ln1_stats(i, j)
                ln1_moments(i, j)
                ln1_var(i, j)
                ln1_norm(i, j)

            ln1(0, 0)
            prep_gt(0, 0)
            maximum(0, 0)
            bias_sum(0, 0)
            bias(0, 0)
            ln1(0, 1)
            dve.wait_ge(s_consts, N_CONSTS)
            def dispatch(g):
                us = slice(g * GU, (g + 1) * GU)
                done = [g * PLAN_STEPS]

                def then(instruction):
                    done[0] += 1
                    instruction.then_inc(s_plan, 1)
                    dve.wait_ge(s_plan, done[0])

                if g == 0:
                    dve.wait_ge(s_tables, 7)
                dve.wait_ge(s_rank, g + 1)
                dve.tensor_copy(rank[:].rearrange("p u e -> p (u e)"), ps_misc[:, 0:GU * E])
                then(dve.tensor_copy(total[:], ps_misc[:, GU * E:2 * GU * E].rearrange("p (u e) -> p e u", e=E)))
                then(dve.tensor_tensor_scan(flat(upto), flat(keep), flat(total), 0.0, ALU.mult, ALU.add))
                then(dve.tensor_tensor(filled[:], upto[:, :, GU - 1:GU].broadcast_to([P, E, GU]),
                                       rows128[:].unsqueeze(1).broadcast_to([P, E, GU]), ALU.is_gt))
                then(dve.tensor_reduce(blocks[:], filled[:], AX.X, ALU.add))
                then(dve.tensor_tensor_scan(blocks_end[:], ones[:, 0:E], blocks[:], 0.0, ALU.mult, ALU.add))
                dve.tensor_tensor(past[:], blocks_end[:].unsqueeze(1).broadcast_to([P, GB, E]),
                                  count_f[:].unsqueeze(2).broadcast_to([P, GB, E]), ALU.is_le)
                then(dve.tensor_tensor(blocks[:], blocks_end[:], blocks[:], ALU.subtract))
                dve.tensor_reduce(owner_f[:], past[:], AX.X, ALU.add)
                then(dve.tensor_tensor(first[:], upto[:], total[:], ALU.subtract))
                then(dve.scalar_tensor_tensor(first[:], blocks[:].unsqueeze(2).broadcast_to([P, E, GU]), float(P), first[:],
                                              ALU.mult, ALU.add))
                dve.tensor_scalar(owner[:, g * GB:(g + 1) * GB], owner_f[:], E - 1.0, None, ALU.min).then_inc(s_owner, 1)
                then(dve.tensor_tensor(spot[:], rank[:], first[:].rearrange("p e u -> p u e"), ALU.add))
                for c in range(TOP_K):
                    last = dve.tensor_tensor(spot_k[:, c], hot[:, c, us], spot[:], ALU.mult)
                then(last)
                then(dve.tensor_reduce(place_f[:], spot_k[:], AX.X, ALU.add))
                dve.tensor_copy(place[:, :, us], place_f[:]).then_inc(s_place, 1)
                assert done[0] == (g + 1) * PLAN_STEPS

            def flat(t):
                return t[:].rearrange("p a b -> p (a b)")

            slots(dve, slot, lambda: dispatch(0))
            dispatch(1)

            def step(i, k):
                m = SB * i + k
                if is_block(m):
                    dve.wait_ge(s_th, m + 1)
                    dve.scalar_tensor_tensor(sg[:, k % 2], th[:, k % 2], 1.0, ps[:, 2 + k % 2, H:H2], ALU.add,
                                             ALU.mult).then_inc(s_sg, 1)
                    dve.wait_ge(s_sg, m + 1)
                    wait(dve, s_ht, m - 1)
                    dve.scalar_tensor_tensor(hid[:, k % 2], sg[:, k % 2], 0.5, ps[:, 2 + k % 2, 0:H], ALU.mult,
                                             ALU.mult).then_inc(s_h, 1)
                if is_block(m - 2):
                    i2, k2 = shift(i, k, -2, SB)
                    dve.wait_ge(s_down, m - 1)
                    if k2 % CH == 0:
                        wait(dve, s_ybuf[k2 // CH], 16 * i2)
                    dve.tensor_copy(blk_y[:, k2 // CH, k2 % CH], ps[:, 6 + k % 2, 0:D]).then_inc(s_y2, 1)

            steps(dve, step)

            for u in range(UNITS):
                g, n = u // GU, u % GU
                dve.wait_ge(s_got[n], 16 * TOP_K * (g + 1))
                dve.scalar_tensor_tensor(base_all[:, u], got[:, n, 0], gate_all[:, u, 0:1], base_all[:, u], ALU.mult,
                                         ALU.add).then_inc(s_part, 1)
                dve.wait_ge(s_part, u + 1)
                dve.scalar_tensor_tensor(base_all[:, u], got[:, n, 1], gate_all[:, u, 1:2], base_all[:, u], ALU.mult,
                                         ALU.add).then_inc(s_final, 1)

        @block.tensor
        def _(pe):
            pe.wait_ge(s_consts, N_CONSTS)
            pe.wait_ge(s_ident, 1)

            def prep_xt(i, j, routed):
                b = 2 * i + j
                pe.wait_ge(s_xn1, b + 1)
                wait(pe, s_lg, routed)
                wait(pe, s_qbk, b)
                for t in range(QT):
                    last = pe.transpose(ps_misc[:, t * P:(t + 1) * P], xn1[:, j, t], ident[:])
                last.then_inc(s_xt, 1)

            def prep_qt(i, j):
                b = 2 * i + j
                pe.wait_ge(s_xtc, b + 1)
                pe.matmul(ps_misc[:, 0:SQ], wq_sb[:], xt_sb[:], start=True, stop=True).then_inc(s_qt, 1)

            def prep_gt(i, j):
                b = 2 * i + j
                pe.wait_ge(s_qtc, b + 1)
                pe.matmul(ps_misc[:, 0:SQ], wkt_sb[:], qt_sb[:], start=True, stop=True)
                for t in range(QT):
                    last = pe.matmul(ps_misc[:, SQ + t:SQ + t + 1], qt_sb[:, t * P:(t + 1) * P], bk_col[:],
                                     start=True, stop=True)
                last.then_inc(s_gt, 1)

            def score(i, k):
                u = 4 * i + k
                j = k // 2
                pe.wait_ge(s_gtc, 2 * i + j + 1)
                pe.wait_ge(s_ctxt[j], 16 * (i + 1))
                wait(pe, s_max, u)
                for c in range(0, SK, BANK):
                    n = min(BANK, SK - c)
                    last = pe.matmul(ps_scores[:, c:c + n], gt_sb[:, j, (k % 2) * P:(k % 2 + 1) * P],
                                     ctxt_sb[:, j, c:c + n], start=True, stop=True)
                last.then_inc(s_scores, 1)

            def turn(i, k, g):
                u = 4 * i + k
                if g == 0:
                    pe.wait_ge(s_exp, u + 1)
                if g < 2:
                    wait(pe, *((s_pt_act, 3 * u) if g == 0 else (s_pt_dve, u)))
                else:
                    pe.wait_ge(s_pt_act, 3 * u + g - 1)
                for t in range(4 * g, min(4 * g + 4, KT)):
                    n = batch_part(t)
                    last = pe.transpose(ps_turn[0:n, g % 2, (t - 4 * g) * P:(t - 4 * g + 1) * P],
                                        probs[:, k % 2, t * P:t * P + n], ident[:])
                last.then_inc(s_turned, 1)

            def times_ctx(i, k, g):
                u = 4 * i + k
                j = k // 2
                if g == 0:
                    pe.wait_ge(s_ctx[j], 32 * (i + 1))
                    wait(pe, s_x1, u)
                if g < GROUPS - 1:
                    pe.wait_ge(s_pt_act, 3 * u + g + 1)
                else:
                    pe.wait_ge(s_pt_dve, u + 1)
                for t in range(4 * g, min(4 * g + 4, KT)):
                    n = batch_part(t)
                    last = pe.matmul(ps_o[:, 0:P], ctx_sb[0:n, j, t], probs_t[0:n, k % 2, t * P:(t + 1) * P],
                                     start=t == 0, stop=t == KT - 1)
                if g == GROUPS - 1:
                    last.then_inc(s_pv, 1)

            def slot(i, k):
                u = 4 * i + k
                nxt = (i, k // 2 + 1) if k < 2 else (i + 1, 0)
                prep = k % 2 == 0 and is_unit(u + 2)
                if is_unit(u + 1):
                    score(*((i, k + 1) if k < 3 else (i + 1, 0)))
                if is_unit(u - 1):
                    pe.wait_ge(s_ot, u)
                    pe.matmul(ps_o[:, 0:D], o_t[:, (k - 1) % 2], wv_sb[:], start=True, stop=True).then_inc(s_attn, 1)
                if is_unit(u - 3):
                    pe.wait_ge(s_rtc, u - 2)
                    pe.matmul(ps_misc[:, 0:E], xnt[:, (k - 3) % 2], wr_sb[:], start=True, stop=True).then_inc(s_logits, 1)
                if prep:
                    prep_xt(*nxt, u - 2)
                if is_unit(u):
                    turn(i, k, 0)
                    turn(i, k, 1)
                    times_ctx(i, k, 0)
                if prep:
                    prep_qt(*nxt)
                if is_unit(u):
                    turn(i, k, 2)
                    times_ctx(i, k, 1)
                if prep:
                    prep_gt(*nxt)
                if is_unit(u):
                    turn(i, k, 3)
                    times_ctx(i, k, 2)
                    times_ctx(i, k, 3)
                if is_unit(u - 2):
                    pe.wait_ge(s_xn2, u - 1)
                    wait(pe, s_lg, u - 2)
                    if prep:
                        pe.wait_ge(s_qbk, 2 * nxt[0] + nxt[1] + 1)
                    pe.transpose(ps_misc[:, 0:P], xn2[:, (k - 2) % 2], ident[:]).then_inc(s_rt, 1)

            prep_xt(0, 0, 0)
            prep_qt(0, 0)
            prep_gt(0, 0)
            score(0, 0)

            def rank_rows(g):
                pe.wait_ge(s_gates, (g + 1) * GU)
                pe.wait_ge(s_lg, min((g + 1) * GU + 1, UNITS))
                pe.wait_ge(s_rtc, min((g + 1) * GU + 2, UNITS))
                for n, table in enumerate((before, ones)):
                    for c in range(TOP_K):
                        rows = hot[:, c, g * GU:(g + 1) * GU].rearrange("p u e -> p (u e)")
                        last = pe.matmul(ps_misc[:, n * GU * E:(n + 1) * GU * E], table[:], rows, start=c == 0,
                                         stop=c == TOP_K - 1)
                last.then_inc(s_rank, 1)
                pe.wait_ge(s_plan, g * PLAN_STEPS + 1)

            slots(pe, slot, lambda: rank_rows(0))
            rank_rows(1)

            def turn_block(i, k):
                m = SB * i + k
                if k % CH == 0:
                    pe.wait_ge(s_blk[k // CH], 16 * (i + 1))
                wait(pe, s_bxc, m - 1)
                pe.transpose(ps[:, k % 2, 0:P], blk_x[:, k // CH, k % CH], ident[:]).then_inc(s_bxt, 1)

            owner_regs = [pe.alloc_register(f"owner{k}") for k in range(SB)]

            def load_owner(i, k):
                pe.load([owner_regs[k]], owner[0:1, bass.ds(SB * i + k, 1)])

            def expert(k):
                return pe.snap(owner_regs[k], min_val=0, max_val=E - 1)

            def step(i, k):
                m = SB * i + k
                if is_block(m + 1):
                    turn_block(*shift(i, k, 1, SB))
                if is_block(m):
                    e = expert(k)
                    pe.wait_ge(s_bxc, m + 1)
                    wait(pe, s_h, m - 1)
                    pe.matmul(ps[:, 2 + k % 2], blk_xt[:, k % 2], wup_sb[:, bass.ds(e, 1)].rearrange("p a h -> p (a h)"),
                              start=True, stop=True).then_inc(s_up, 1)
                    if is_block(m + 1):
                        load_owner(*shift(i, k, 1, SB))
                if is_block(m - 1):
                    pe.wait_ge(s_h, m)
                    wait(pe, s_htc, m - 2)
                    for c in range(HC):
                        last = pe.transpose(ps[:, 4 + (k - 1) % 2, c * P:(c + 1) * P], hid[:, (k - 1) % 2, c * P:(c + 1) * P],
                                            ident[:])
                    last.then_inc(s_ht, 1)
                if is_block(m - 2):
                    e = expert((k - 2) % SB)
                    pe.wait_ge(s_htc, m - 1)
                    wait(pe, s_y2, m - 3)
                    for c in range(HC):
                        last = pe.matmul(ps[:, 6 + k % 2, 0:D], hid_t[:, k % 2, c * P:(c + 1) * P],
                                         wdn_sb[:, bass.ds(e, 1), c].rearrange("p a d -> p (a d)"),
                                         start=c == 0, stop=c == HC - 1)
                    last.then_inc(s_down, 1)

            pe.wait_ge(s_experts, 32)
            pe.wait_ge(s_max, UNITS)
            pe.wait_ge(s_pt_dve, UNITS)
            pe.wait_ge(s_pt_act, 3 * UNITS)
            pe.wait_ge(s_x1, UNITS)
            pe.wait_ge(s_owner, GROUPS_D)
            load_owner(0, 0)
            turn_block(0, 0)
            steps(pe, step)


def kernel(x, ctx_1024, mask_BxS2_ik0, L0_xattn_Wq, L0_xattn_bq, L0_xattn_Wk, L0_xattn_bk, L0_xattn_Wv,
           L0_xattn_bv, L0_ffn_norm_scale, L0_ffn_w_router, L0_ffn_w_up, L0_ffn_w_down):
    import numpy as np
    import concourse.bacc as bacc
    from concourse.bass_utils import run_bass_kernel_spmd

    def turned(a, *axes):
        return np.ascontiguousarray(np.asarray(a).transpose(*axes))

    arrays = {
        "x": np.ascontiguousarray(x),
        "ctx_rows": np.ascontiguousarray(ctx_1024),
        "ctx_cols": turned(ctx_1024, 0, 2, 1),
        "mask": np.ascontiguousarray(mask_BxS2_ik0),
        "wq": np.ascontiguousarray(L0_xattn_Wq),
        "wk_t": turned(L0_xattn_Wk, 1, 0),
        "wv": np.ascontiguousarray(L0_xattn_Wv),
        "bq": np.asarray(L0_xattn_bq).reshape(-1, 1),
        "bk": np.asarray(L0_xattn_bk).reshape(-1, 1),
        "bv": np.ascontiguousarray(L0_xattn_bv),
        "norm_scale": np.ascontiguousarray(L0_ffn_norm_scale),
        "w_router_t": turned(L0_ffn_w_router, 1, 0),
        "w_up_t": turned(L0_ffn_w_up, 0, 2, 1),
        "w_down_t": turned(L0_ffn_w_down, 0, 2, 1),
    }
    nc = bacc.Bacc("TRN2", target_bir_lowering=False, num_devices=1)
    aps = [nc.dram_tensor(n, a.shape, mybir.dt.from_np(a.dtype), kind="ExternalInput").ap() for n, a in arrays.items()]
    out = nc.dram_tensor("out", arrays["x"].shape, F32, kind="ExternalOutput").ap()
    xattn_moe(nc, *aps, out)
    result = run_bass_kernel_spmd(nc, [arrays], core_ids=[0])
    return result.results[0]["out"]
```

```python
from contextlib import ExitStack

import concourse.bass as bass
from concourse import mybir

F32 = mybir.dt.float32
F32R = mybir.dt.float32r
I32 = mybir.dt.int32
U32 = mybir.dt.uint32
ALU = mybir.AluOpType
ACT = mybir.ActivationFunctionType
AX = mybir.AxisListType

P = 128
LN_EPS = 1e-5
RMS_EPS = 1e-6
MASKED = -1e30
LOWEST = -3.4e38
BANK = 512


def wait(eng, sem, value):
    if not isinstance(value, int) or value > 0:
        eng.wait_ge(sem, value)


def xattn_moe(nc, x, ctx_rows, ctx_cols, mask, wq, wk_t, wv, bq, bk, bv, norm_scale, w_router_t,
              w_up_t, w_down_t, out):
    B, SQ, D = x.shape
    SK = ctx_rows.shape[1]
    E, _, H2 = w_up_t.shape
    H = H2 // 2
    QT = SQ // P
    UNITS = B * QT
    SKE = SK + SK % 2
    TOK = B * SQ
    KT = -(-SK // P)
    TAIL = SK - (KT - 1) * P
    GROUPS = -(-KT // 4)
    HC = H // P
    SCALE = float(D) ** -0.5
    assert D == P and QT == 2 and B % 2 == 0 and B >= 6 and GROUPS == 4 and TAIL < P and HC == 2 and E == 8
    PAIRS = B // 2
    RING = 4
    TOP_K = 2
    GROUPS_D = 2
    GU = [UNITS * 5 // 8, UNITS * 3 // 8]
    GB = [TOP_K * n + E for n in GU]
    NB = sum(GB)
    FIRST_UNIT = [0, GU[0]]
    FIRST_BLOCK = [0, GB[0]]
    ROOM = 24
    GOT = 2
    CH = 4
    SB = 2 * CH
    CHUNKS = [n // CH for n in GB]
    READY = GU[0] + 3
    SPLIT = READY // 4
    SCATTERS = [3, 3]
    assert E == PAIRS and NB % SB == 0 and GB[0] % CH == 0 and CHUNKS[0] % 2 == 0 and 1 < SPLIT < PAIRS

    def batch_part(t):
        return P if t < KT - 1 else TAIL

    x_tiles = x.rearrange("b (t p) d -> b p t d", p=P)
    out_tiles = out.rearrange("b (t p) d -> p (b t) d", p=P)

    rows_in = [nc.dram_tensor(f"rows_in{g}", [GB[g] * P, D], F32, kind="Internal").ap() for g in range(GROUPS_D)]
    rows_out = [nc.dram_tensor(f"rows_out{g}", [GB[g] * P, D], F32, kind="Internal").ap() for g in range(GROUPS_D)]
    mbias_dram = nc.dram_tensor("mbias_dram", [B, SK], F32, kind="Internal").ap()

    st = ExitStack()
    with st:
        def sb(name, shape, dt=F32):
            return st.enter_context(nc.sbuf_tensor(name, shape, dt))

        def sem(name):
            return st.enter_context(nc.semaphore(name))

        wq_sb = sb("wq_sb", [P, D])
        wkt_sb = sb("wkt_sb", [P, D])
        wv_sb = sb("wv_sb", [P, D])
        wr_sb = sb("wr_sb", [P, E])
        wup_in = sb("wup_in", [P, H2])
        wup_high = sb("wup_high", [P, E, H2], F32R)
        wup_low = sb("wup_low", [P, E, H2], F32R)
        wdn_sb = sb("wdn_sb", [P, E, HC, D])
        bq_col = sb("bq_col", [P, 1])
        bk_col = sb("bk_col", [P, 1])
        bv_rows = sb("bv_rows", [P, D])
        norm_rows = sb("norm_rows", [P, D])
        ident = sb("ident", [P, P])
        spare = sb("spare", [P, 8])
        minus_half = sb("minus_half", [P, 2])
        iota_i = sb("iota_i", [P, E], I32)
        iota_f = sb("iota_f", [P, E])
        x_in = sb("x_in", [P, 2, QT, D])
        xn1 = sb("xn1", [P, 2, QT, D])
        ctx_sb = sb("ctx_sb", [P, 2, KT, D])
        ctxt_in = sb("ctxt_in", [P, SK])
        ctxt_high = sb("ctxt_high", [P, 2, SKE], F32R)
        ctxt_low = sb("ctxt_low", [P, 2, SKE], F32R)
        mask_i = sb("mask_i", [B, SK], I32)
        mbias_rows = sb("mbias_rows", [B, SK])
        mbias = sb("mbias", [P, 2, SK])
        xt_sb = sb("xt_sb", [P, SQ])
        qt_sb = sb("qt_sb", [P, SQ])
        gt_high = sb("gt_high", [P, 2, SQ], F32R)
        gt_low = sb("gt_low", [P, 2, SQ], F32R)
        qbk = sb("qbk", [P, 2, QT])
        st1 = sb("st1", [P, QT, 6])
        mv1 = sb("mv1", [P, QT, 2])
        ve1 = sb("ve1", [P, QT])
        rstd1 = sb("rstd1", [P, QT])
        attention = sb("attention", [P, max(3 * SK + KT * P, ROOM * TOP_K * D)])
        scores = attention[:, 0:SK]
        probs = attention[:, SK:3 * SK].rearrange("p (a n) -> p a n", a=2)
        probs_t = attention[:, 3 * SK:3 * SK + KT * P]
        smax = sb("smax", [P, RING])
        smax2 = sb("smax2", [P, RING])
        ebias = sb("ebias", [P, RING])
        esum = sb("esum", [P, RING])
        rsum = sb("rsum", [P, RING])
        o_t = sb("o_t", [P, 2, P])
        x1 = sb("x1", [P, RING, D])
        st2 = sb("st2", [P, 6])
        mv2 = sb("mv2", [P, 2])
        ve2 = sb("ve2", [P, 2])
        rstd2 = sb("rstd2", [P, 2])
        y = sb("y", [P, 2, D])
        xc = sb("xc", [P, D])
        warm = sb("warm", [P, 1])
        xn2 = sb("xn2", [P, 2, D])
        xnt = sb("xnt", [P, 2, P])
        logits = sb("logits", [P, E])
        top = sb("top", [P, 8])
        top_i = sb("top_i", [P, 8], U32)
        top_f = sb("top_f", [P, 2, 2])
        sdiff = sb("sdiff", [P, 1])
        e2 = sb("e2", [P, 2, 1])
        den = sb("den", [P, 1])
        hot = sb("hot", [P, TOP_K, UNITS, E])
        gate_all = sb("gate_all", [P, UNITS, TOP_K])
        xn2_all = sb("xn2_all", [P, UNITS, D])
        base_all = sb("base_all", [P, UNITS, D])
        place = sb("place", [P, TOP_K, UNITS], I32)
        ones = sb("ones", [P, P])
        before = sb("before", [P, P])
        zeros = sb("zeros", [P, D])
        keep = [sb(f"keep{g}", [P, E, GU[g]]) for g in range(GROUPS_D)]
        count_i = sb("count_i", [P, GB[0]], I32)
        count_f = sb("count_f", [P, GB[0]])
        rows128 = sb("rows128", [P, GU[0]])
        rank = sb("rank", [P, GU[0] * E])
        total = sb("total", [P, E * GU[0]])
        upto = sb("upto", [P, E * GU[0]])
        filled = sb("filled", [P, E * GU[0]])
        blocks = sb("blocks", [P, E])
        blocks_end = sb("blocks_end", [P, E])
        first = sb("first", [P, E * GU[0]])
        spot = sb("spot", [P, GU[0] * E])
        spot_k = sb("spot_k", [P, TOP_K, GU[0] * E])
        place_f = sb("place_f", [P, TOP_K, GU[0]])
        past = sb("past", [P, GB[0], E])
        owner_f = sb("owner_f", [P, GB[0]])
        owner = sb("owner", [P, NB], I32)
        blk_x = sb("blk_x", [P, 2, CH, D])
        xt_high = sb("xt_high", [P, 2, P], F32R)
        xt_low = sb("xt_low", [P, 2, P], F32R)
        inner = ctx_sb[:].rearrange("p a t d -> p (a t d)")[:, 0:4 * 2 * H].rearrange("p (s j h) -> p s j h", s=4, j=2)
        th, sg, hid, hid_t = inner[:, 0], inner[:, 1], inner[:, 2], inner[:, 3]
        blk_y = mbias[:].rearrange("p a n -> p (a n)")[:, 0:2 * CH * D].rearrange("p (j t d) -> p j t d", j=2, t=CH)
        got = attention[:, 0:ROOM * TOP_K * D].rearrange("p (u c d) -> p u c d", u=ROOM, c=TOP_K)

        ps = st.enter_context(nc.psum_tensor("ps", [P, 8, BANK], F32))
        ps_scores = ps[:, 0:4, :].rearrange("p a b -> p (a b)")
        ps_turn = ps[:, 4:6, :]
        ps_o = ps[:, 6, :]
        ps_misc = ps[:, 7, :]

        s_consts_qk = sem("query_key_consts_loaded")
        s_consts = sem("other_consts_loaded")
        s_wdn = sem("down_weights_loaded")
        s_wup = sem("up_weights_loaded")
        s_wup_high = sem("up_weights_high")
        s_wup_low = sem("up_weights_low")
        s_mbias = [sem(f"mbias_loaded{j}") for j in range(2)]
        s_x = [sem(f"x_loaded{j}") for j in range(2)]
        s_ctx = [sem(f"ctx_loaded{j}") for j in range(2)]
        s_ctxt = sem("ctxt_loaded")
        s_ctxt_high = sem("ctxt_high")
        s_ctxt_low = sem("ctxt_low")
        s_mask = sem("mask_loaded")
        s_mrows = sem("mask_bias_made")
        s_mstore = sem("mask_bias_stored")
        s_stored = sem("stored")
        s_cleared = [sem(f"rows_cleared{g}") for g in range(GROUPS_D)]
        s_blk = [sem(f"block_rows_loaded{j}") for j in range(2)]
        s_ybuf = [sem(f"result_buffer_stored{j}") for j in range(2)]
        s_scat = [sem(f"rows_scattered{g}") for g in range(GROUPS_D)]
        s_got = [sem(f"rows_gathered{n}") for n in range(UNITS // GOT)]
        s_pool = sem("pool_consts_set")
        s_ident = sem("ident_ready")
        s_xb = sem("x_plus_bv_ready")
        s_base = sem("base_ready")
        s_keep = sem("xn2_kept")
        s_zeros = sem("zeros_set")
        s_pad = sem("ctxt_pad_set")
        s_tables = sem("dispatch_tables_set")
        s_scores = sem("scores_ready")
        s_turned = sem("probs_turned")
        s_pv = sem("pv_done")
        s_attn = sem("attn_ready")
        s_xt = sem("xt_ready")
        s_qt = sem("qt_ready")
        s_gt = sem("gt_ready")
        s_rt = sem("rt_ready")
        s_logits = sem("logits_ready")
        s_rank = sem("rank_ready")
        s_bxt = sem("block_turned")
        s_up = sem("up_ready")
        s_ht = sem("hidden_turned")
        s_down = sem("down_ready")
        s_exp = sem("exp_done")
        s_pt_act = sem("probs_t_by_act")
        s_ot = sem("o_t_ready")
        s_xtc = sem("xt_copied")
        s_qtc = sem("qt_copied")
        s_rtc = sem("rt_copied")
        s_e2 = sem("e2_ready")
        s_xt_high = sem("block_turned_high")
        s_xt_low = sem("block_turned_low")
        s_htc = sem("hidden_turned_copied")
        s_th = sem("tanh_ready")
        s_iota = sem("iota_ready")
        s_max = sem("max_done")
        s_max2 = sem("max2_done")
        s_ebias = sem("ebias_ready")
        s_gth = sem("gt_high_copied")
        s_gtc = sem("gt_split")
        s_qbk = sem("qbk_copied")
        s_pt_dve = sem("probs_t_by_dve")
        s_rsum = sem("rsum_ready")
        s_x1 = sem("x1_ready")
        s_st1 = sem("ln1_stats")
        s_mv1 = sem("ln1_moments")
        s_ve1 = sem("ln1_var_eps")
        s_rs1 = sem("ln1_rstd")
        s_xn1 = sem("xn1_ready")
        s_st2 = sem("ln2_stats")
        s_mv2 = sem("ln2_moments")
        s_ve2 = sem("ln2_var_eps")
        s_rs2 = sem("ln2_rstd")
        s_y = sem("y_ready")
        s_xc = sem("xc_ready")
        s_xn2 = sem("xn2_ready")
        s_lg = sem("logits_copied")
        s_top = sem("top_ready")
        s_topi = sem("top_index_ready")
        s_sd = sem("sdiff_ready")
        s_topf = sem("top_f_ready")
        s_den = sem("den_ready")
        s_w1 = sem("gate1_ready")
        s_gates = sem("gates_ready")
        s_sg = sem("sg_ready")
        s_h = sem("h_ready")
        s_y2 = sem("block_result_ready")
        s_plan = sem("dispatch_step")
        s_place = sem("places_ready")
        PLAN_STEPS = 13
        s_owner = sem("owners_ready")
        s_part = sem("first_choice_added")
        s_final = sem("result_ready")

        block = st.enter_context(nc.Block())

        def is_unit(u):
            return not isinstance(u, int) or 0 <= u < UNITS

        def is_block(m):
            return not isinstance(m, int) or 0 <= m < NB

        def run(eng, slot, first_group, before_steps, step, second_group):
            for k in range(4):
                slot(0, k)
            with eng.Fori(1, SPLIT) as i:
                for k in range(4):
                    slot(i, k)
            for n in range(4 * SPLIT, UNITS):
                for part in first_group.get(n - READY, ()):
                    part(0)
                slot(n // 4, n % 4)
            before_steps()
            slot(PAIRS, 0)
            for k in range(SB):
                step(0, k)
                if k < 2:
                    slot(PAIRS, k + 1)
                for part in second_group.get(k, ()):
                    part(1)
            with eng.Fori(1, NB // SB - 1) as i:
                for k in range(SB):
                    step(i, k)
            for k in range(SB):
                step(NB // SB - 1, k)
            for k in range(3):
                step(NB // SB, k)

        def shift(i, k, d, n):
            return (i, k + d) if 0 <= k + d < n else (i + (1 if d > 0 else -1), k + d - (n if d > 0 else -n))

        @block.sync
        def _(sp):
            def load(i, j):
                b = 2 * i + j
                wait(sp, s_xn1, b - 1)
                wait(sp, s_xb, b - 1)
                sp.dma_start(x_in[:, j], x_tiles[b]).then_inc(s_x[j], 16)
                wait(sp, s_ctxt_low, b)
                sp.dma_start(ctxt_in[:], ctx_cols[b]).then_inc(s_ctxt, 16)
                if isinstance(i, int) and b == 0:
                    sp.wait_ge(s_mstore, 16)
                wait(sp, s_max, QT * (b - 1))
                sp.dma_start(mbias[:, j], mbias_dram[b].partition_broadcast(P)).then_inc(s_mbias[j], 16)
                wait(sp, s_pv, QT * (b - 1))
                sp.dma_start(ctx_sb[:, j, 0:KT - 1],
                             ctx_rows[b][0:(KT - 1) * P].rearrange("(t p) d -> p t d", p=P)).then_inc(s_ctx[j], 16)
                sp.dma_start(ctx_sb[0:TAIL, j, KT - 1], ctx_rows[b][(KT - 1) * P:SK]).then_inc(s_ctx[j], 16)

            def load_expert(e):
                wait(sp, s_wup_low, e)
                sp.dma_start(wup_in[:].unsqueeze(1), w_up_t[bass.ds(e, 1)].rearrange("e d h -> d e h")).then_inc(s_wup, 16)
                sp.dma_start(wdn_sb[:, bass.ds(e, 1)],
                             w_down_t[bass.ds(e, 1)].rearrange("e (c p) d -> p e c d", p=P)).then_inc(s_wdn, 16)

            sp.dma_start(mask_i[:], mask).then_inc(s_mask, 16)
            for dst, src in ((wq_sb[:], wq), (wkt_sb[:], wk_t), (bq_col[:], bq), (bk_col[:], bk)):
                sp.dma_start(dst, src).then_inc(s_consts_qk, 16)
            load(0, 0)
            for dst, src in ((wv_sb[:], wv), (wr_sb[:], w_router_t), (bv_rows[:], bv.partition_broadcast(P)),
                             (norm_rows[:], norm_scale.partition_broadcast(P))):
                sp.dma_start(dst, src).then_inc(s_consts, 16)
            load(0, 1)
            load_expert(0)
            sp.wait_ge(s_zeros, 1)
            ends = [1, PAIRS // 2, PAIRS]
            for g in range(GROUPS_D):
                pieces = 2 * (ends[g + 1] - ends[g])
                assert GB[g] % pieces == 0
                cleared = rows_in[g].rearrange("(c n p) d -> c p n d", c=pieces, p=P)
                with sp.Fori(ends[g], ends[g + 1]) as i:
                    for j in range(2):
                        load(i, j)
                        sp.dma_start(cleared[2 * (i - ends[g]) + j],
                                     zeros[:].unsqueeze(1).broadcast_to([P, GB[g] // pieces, D])).then_inc(s_cleared[g], 16)
                        if j == 1:
                            load_expert(i)

            in_chunks = [t.rearrange("(c t p) d -> c p t d", t=CH, p=P) for t in rows_in]
            out_chunks = [t.rearrange("(c t p) d -> c p t d", t=CH, p=P) for t in rows_out]

            def load_chunk(c, i, j):
                g = 0 if c < CHUNKS[0] else 1
                wait(sp, s_bxt, CH * (2 * i + j - 1))
                sp.dma_start(blk_x[:, j], in_chunks[g][2 * i + j - g * CHUNKS[0]]).then_inc(s_blk[j], 16)

            def store_chunk(c, i, j):
                g = 0 if c < CHUNKS[0] else 1
                sp.wait_ge(s_y2, CH * (2 * i + j + 1))
                sp.dma_start(out_chunks[g][2 * i + j - g * CHUNKS[0]], blk_y[:, j]).then_inc(s_ybuf[j], 16)

            def chunk_pairs(i, n):
                with sp.Fori(i, n) as i2:
                    for j in range(2):
                        load_chunk(2 * i + 2, i2 + 1, j)
                        store_chunk(2 * i, i2, j)

            sp.wait_ge(s_scat[0], 16 * TOP_K * GU[0])
            for j in range(2):
                load_chunk(j, 0, j)
            LAST, END = CHUNKS[0] // 2, sum(CHUNKS) // 2
            chunk_pairs(0, LAST - 1)
            sp.wait_ge(s_scat[1], 16 * TOP_K * GU[1])
            for j in range(2):
                load_chunk(2 * LAST + j, LAST, j)
                store_chunk(2 * LAST - 2 + j, LAST - 1, j)
            chunk_pairs(LAST, END - 1)
            for j in range(2):
                store_chunk(2 * END - 2 + j, END - 1, j)

            for u in range(0, UNITS, 4):
                sp.wait_ge(s_final, u + 4)
                sp.dma_start(out_tiles[:, u:u + 4], base_all[:, u:u + 4]).then_inc(s_stored, 16)
            sp.wait_ge(s_stored, 16 * UNITS // 4)

        N_CONSTS = 4 * 16

        @block.gpsimd
        def _(pool):
            def make_xb(i, j):
                b = 2 * i + j
                pool.wait_ge(s_x[j], 16 * (i + 1))
                wait(pool, s_base, QT * (b - 1))
                wait(pool, s_xn2, QT * (b - 1))
                for t in range(QT):
                    last = pool.tensor_tensor(x1[:, 2 * j + t], x_in[:, j, t], bv_rows[:], ALU.add)
                last.then_inc(s_xb, 1)

            def rstd_of_x(i, j):
                pool.wait_ge(s_ve1, 2 * i + j + 1)
                wait(pool, s_xn1, 2 * i + j)
                pool.tensor_tensor(rstd1[:], ve1[:], minus_half[:], ALU.pow).then_inc(s_rs1, 1)

            def slot_first(i, k):
                u = 4 * i + k
                if is_unit(u - 2):
                    pool.wait_ge(s_y, u - 1)
                    pool.tensor_tensor(base_all[:, bass.ds(u - 2, 1)],
                                       x1[:, (k - 2) % 4:(k - 2) % 4 + 1], y[:, (k - 2) % 2:(k - 2) % 2 + 1],
                                       ALU.add).then_inc(s_base, 1)
                if k % 2 == 1 and is_unit(u + 3):
                    rstd_of_x(i + 1, k // 2)
                if k == 3 and is_unit(u + 1):
                    make_xb(i + 1, 0)
                if k == 1 and is_unit(u):
                    make_xb(i, 1)

            def slot_second(i, k):
                u = 4 * i + k
                if is_unit(u - 1):
                    pool.wait_ge(s_ve2, u)
                    wait(pool, s_xn2, u - 1)
                    pool.tensor_tensor(rstd2[:], ve2[:], minus_half[:], ALU.pow).then_inc(s_rs2, 1)

            def scatter(g, n):
                u, c = FIRST_UNIT[g] + n // TOP_K, n % TOP_K
                if n == 0:
                    pool.wait_ge(s_cleared[g], 16 * 2 * (PAIRS // 2 - 1 if g == 0 else PAIRS - PAIRS // 2))
                    pool.wait_ge(s_place, g + 1)
                    pool.wait_ge(s_keep, FIRST_UNIT[g] + GU[g])
                pool.indirect_dma_start(rows_in[g], bass.IndirectOffsetOnAxis(ap=place[:, c, u:u + 1], axis=0),
                                        xn2_all[:, u], None).then_inc(s_scat[g], 16)

            pool.memset(zeros[:], 0.0).then_inc(s_zeros, 1)
            for part in (ctxt_high, ctxt_low):
                pool.memset(part[:, :, SK:SKE].bitcast(F32), 0.0).then_inc(s_pad, 1)
            pool.memset(ident[:], 0.0).then_inc(s_pool, 1)
            pool.memset(minus_half[:], -0.5).then_inc(s_pool, 1)
            pool.iota(iota_i[:], pattern=[[1, E]], base=0, channel_multiplier=0).then_inc(s_pool, 1)
            pool.wait_ge(s_pool, 3)
            pool.affine_select(out=ident[:], in_=ident[:], compare_op=ALU.not_equal, fill=1.0, base=0,
                               pattern=[[-1, P]], channel_multiplier=1).then_inc(s_ident, 1)
            pool.tensor_copy(iota_f[:], iota_i[:]).then_inc(s_iota, 1)
            rstd_of_x(0, 0)
            rstd_of_x(0, 1)
            pool.memset(ones[:], 1.0).then_inc(s_tables, 1)
            for g in range(GROUPS_D):
                pool.memset(keep[g][:], 1.0).then_inc(s_tables, 1)
            pool.iota(count_i[:], pattern=[[1, GB[0]]], base=0, channel_multiplier=0).then_inc(s_tables, 1)
            pool.wait_ge(s_tables, 4)
            for g in range(GROUPS_D):
                pool.memset(keep[g][:, :, 0:1], 0.0).then_inc(s_tables, 1)
            pool.affine_select(out=before[:], in_=ones[:], compare_op=ALU.is_gt, fill=0.0, base=0,
                               pattern=[[1, P]], channel_multiplier=-1).then_inc(s_tables, 1)
            pool.tensor_copy(count_f[:], count_i[:]).then_inc(s_tables, 1)
            pool.wait_ge(s_tables, 8)
            pool.tensor_scalar(rows128[:], count_f[:, 0:GU[0]], float(P), None, ALU.mult).then_inc(s_tables, 1)
            pool.wait_ge(s_consts, N_CONSTS)
            make_xb(0, 0)

            for k in range(4):
                slot_first(0, k)
                slot_second(0, k)
            with pool.Fori(1, SPLIT) as i:
                for k in range(4):
                    slot_first(i, k)
                    slot_second(i, k)
            def scatters(sent, n):
                end = min(sent + n, TOP_K * GU[0])
                for n in range(sent, end):
                    scatter(0, n)
                return end

            sent = 0
            for i in range(SPLIT, PAIRS + 1):
                for k in range(4):
                    slot_first(i, k)
                    if READY < 4 * i + k:
                        sent = scatters(sent, SCATTERS[0])
                    slot_second(i, k)
                    if READY <= 4 * i + k < UNITS:
                        sent = scatters(sent, SCATTERS[1])
            assert sent == TOP_K * GU[0]
            for n in range(TOP_K * GU[1]):
                scatter(1, n)
            for u in range(UNITS):
                g = 0 if u < GU[0] else 1
                if u == FIRST_UNIT[g]:
                    for j in range(2):
                        pool.wait_ge(s_ybuf[j], 16 * sum(CHUNKS[:g + 1]) // 2)
                if u == 0:
                    pool.wait_ge(s_exp, UNITS)
                    pool.wait_ge(s_turned, GROUPS * UNITS)
                    pool.wait_ge(s_pv, UNITS)
                wait(pool, s_final, u - ROOM + 1)
                for c in range(TOP_K):
                    pool.indirect_dma_start(got[:, u % ROOM, c], None, rows_out[g],
                                            bass.IndirectOffsetOnAxis(ap=place[:, c, u:u + 1], axis=0)).then_inc(s_got[u // GOT], 16)

        @block.scalar
        def _(act):
            act.wait_ge(s_pool, 3)
            act.activation(warm[:], minus_half[:, 0:1], ACT.Exp)
            act.wait_ge(s_mrows, 1)
            act.dma_start(mbias_dram, mbias_rows[:]).then_inc(s_mstore, 16)
            act.wait_ge(s_consts_qk, N_CONSTS)

            def prep_xt(i, j):
                b = 2 * i + j
                act.wait_ge(s_xt, b + 1)
                wait(act, s_qt, b)
                act.activation(xt_sb[:], ps_misc[:, 0:SQ], ACT.Copy).then_inc(s_xtc, 1)

            def prep_qt(i, j):
                b = 2 * i + j
                act.wait_ge(s_qt, b + 1)
                wait(act, s_gt, b)
                act.activation(qt_sb[:], ps_misc[:, 0:SQ], ACT.Identity, bias=bq_col[:]).then_inc(s_qtc, 1)

            def exp_unit(i, k):
                u = 4 * i + k
                act.wait_ge(s_ebias, u + 1)
                wait(act, s_turned, GROUPS * (u - 1))
                wait(act, s_rsum, u - 3)
                act.activation(probs[:, k % 2], scores, ACT.Exp, bias=ebias[:, k:k + 1], scale=SCALE,
                               accum_out=esum[:, k:k + 1]).then_inc(s_exp, 1)

            def slot(i, k):
                u = 4 * i + k
                nxt = (i, k // 2 + 1) if k < 2 else (i + 1, 0)
                prep = k % 2 == 0 and is_unit(u + 2)
                if k % 2 == 1 and is_unit(u + 3):
                    split_ctxt(i + 1, k // 2)
                if is_unit(u - 2):
                    act.wait_ge(s_rt, u - 1)
                    wait(act, s_logits, u - 3)
                    act.activation(xnt[:, k % 2], ps_misc[:, 0:P], ACT.Copy).then_inc(s_rtc, 1)
                    act.activation(xn2_all[:, bass.ds(u - 2, 1)], xn2[:, k % 2:k % 2 + 1], ACT.Copy).then_inc(s_keep, 1)
                wait(act, s_pv, min(u, UNITS) if isinstance(u, int) else u)
                for g in range(GROUPS - 1):
                    if is_unit(u):
                        act.wait_ge(s_turned, GROUPS * u + g + 1)
                        act.activation(probs_t[:, g * BANK:(g + 1) * BANK], ps_turn[:, g % 2],
                                       ACT.Copy).then_inc(s_pt_act, 1)
                    if prep and g < 2:
                        (prep_xt, prep_qt)[g](*nxt)
                if is_unit(u + 1):
                    exp_unit(*((i, k + 1) if k < 3 else (i + 1, 0)))
                if is_unit(u):
                    act.wait_ge(s_pv, u + 1)
                    wait(act, s_attn, u - 1)
                    act.activation(o_t[:, k % 2], ps_o[:, 0:P], ACT.Copy).then_inc(s_ot, 1)
                if is_unit(u - 2):
                    act.wait_ge(s_sd, u - 1)
                    wait(act, s_gates, u - 3)
                    act.activation(e2[:, (k - 2) % 2], sdiff[:], ACT.Exp).then_inc(s_e2, 1)
                if k == 1 and is_unit(u):
                    split_up_weights(i)

            def split_ctxt(i, j):
                b = 2 * i + j
                act.wait_ge(s_ctxt, 16 * (b + 1))
                wait(act, s_scores, QT * (b - 1))
                act.activation(ctxt_high[:, j, 0:SK], ctxt_in[:], ACT.Copy).then_inc(s_ctxt_high, 1)

            def split_up_weights(e):
                act.wait_ge(s_wup, 16 * (e + 1))
                act.activation(wup_high[:, bass.ds(e, 1)], wup_in[:].unsqueeze(1), ACT.Copy).then_inc(s_wup_high, 1)

            prep_xt(0, 0)
            prep_qt(0, 0)
            split_ctxt(0, 0)
            exp_unit(0, 0)
            split_ctxt(0, 1)


            def block_xt(i, k):
                m = SB * i + k
                act.wait_ge(s_bxt, m + 1)
                wait(act, s_up, m - 1)
                act.activation(xt_high[:, k % 2], ps[:, 0, 0:P], ACT.Copy).then_inc(s_xt_high, 1)

            def step(i, k):
                m = SB * i + k
                if is_block(m + 1):
                    block_xt(*shift(i, k, 1, SB))
                if is_block(m):
                    act.wait_ge(s_up, m + 1)
                    wait(act, s_sg, m - 1)
                    act.activation(th[:, k % 2], ps[:, 2 + k % 2, H:H2], ACT.Tanh, scale=0.5).then_inc(s_th, 1)
                if is_block(m - 2):
                    act.wait_ge(s_ht, m - 1)
                    wait(act, s_down, m - 3)
                    act.activation(hid_t[:, k % 2], ps[:, 4 + k % 2, 0:HC * P], ACT.Copy).then_inc(s_htc, 1)
                if is_block(m - 3):
                    i2, k2 = shift(i, k, -3, SB)
                    act.wait_ge(s_down, m - 2)
                    if k2 % CH == 0:
                        wait(act, s_ybuf[k2 // CH], 16 * i2)
                    act.activation(blk_y[:, k2 // CH, k2 % CH], ps[:, (1, 6)[k % 2], 0:D], ACT.Copy).then_inc(s_y2, 1)

            run(act, slot, {}, lambda: block_xt(0, 0), step, {})

        @block.vector
        def _(dve):
            def take_waits(n):
                dve.memset(spare[:, n:n + 1], 0.0)


            def ln1_stats(i, j):
                dve.wait_ge(s_x[j], 16 * (i + 1))
                for t in range(QT):
                    last = dve.bn_stats(st1[:, t], x_in[:, j, t])
                last.then_inc(s_st1, 1)

            def ln1_moments(i, j):
                dve.wait_ge(s_st1, 2 * i + j + 1)
                take_waits(0)
                for t in range(QT):
                    last = dve.bn_aggr(mv1[:, t], st1[:, t])
                last.then_inc(s_mv1, 1)

            def ln1_var(i, j):
                dve.wait_ge(s_mv1, 2 * i + j + 1)
                dve.tensor_scalar(ve1[:], mv1[:, :, 1], LN_EPS, None, ALU.add).then_inc(s_ve1, 1)

            def ln1_norm(i, j):
                b = 2 * i + j
                dve.wait_ge(s_rs1, b + 1)
                wait(dve, s_xt, b - 1)
                for t in range(QT):
                    last = dve.tensor_scalar(xn1[:, j, t], x_in[:, j, t], mv1[:, t, 0:1], rstd1[:, t:t + 1],
                                             ALU.subtract, ALU.mult)
                last.then_inc(s_xn1, 1)

            def prep_gt(i, j):
                b = 2 * i + j
                dve.wait_ge(s_gt, b + 1)
                wait(dve, s_scores, QT * (b - 1))
                dve.tensor_copy(gt_high[:, j], ps_misc[:, 0:SQ]).then_inc(s_gth, 1)
                wait(dve, s_ebias, QT * (b - 1))
                dve.tensor_copy(qbk[:, j], ps_misc[:, SQ:SQ + QT]).then_inc(s_qbk, 1)
                dve.wait_ge(s_gth, b + 1)
                dve.tensor_tensor(gt_low[:, j], ps_misc[:, 0:SQ], gt_high[:, j].bitcast(F32),
                                  ALU.subtract).then_inc(s_gtc, 1)

            def maximum(i, k):
                u = 4 * i + k
                j = k // 2
                dve.wait_ge(s_scores, u + 1)
                dve.wait_ge(s_mbias[j], 16 * (i + 1))
                wait(dve, s_exp, u)
                take_waits(1)
                dve.tensor_tensor_reduce(out=scores, in0=ps_scores[:, 0:SK], in1=mbias[:, j], scale=1.0,
                                         scalar=LOWEST, op0=ALU.add, op1=ALU.max,
                                         accum_out=smax[:, k:k + 1]).then_inc(s_max, 1)

            def bias_sum(i, k):
                u = 4 * i + k
                j = k // 2
                dve.wait_ge(s_max, u + 1)
                dve.wait_ge(s_qbk, 2 * i + j + 1)
                dve.tensor_scalar(smax2[:, k:k + 1], smax[:, k:k + 1], qbk[:, j, k % 2:k % 2 + 1], -SCALE, ALU.add,
                                  ALU.mult).then_inc(s_max2, 1)

            def bias(i, k):
                u = 4 * i + k
                dve.wait_ge(s_max2, u + 1)
                dve.scalar_tensor_tensor(ebias[:, k:k + 1], qbk[:, k // 2, k % 2:k % 2 + 1], SCALE, smax2[:, k:k + 1],
                                         ALU.mult, ALU.add).then_inc(s_ebias, 1)

            def post_sum(i, kk):
                u = 4 * i + kk
                r = kk % RING
                dve.wait_ge(s_exp, u + 1)
                dve.reciprocal(rsum[:, r:r + 1], esum[:, r:r + 1]).then_inc(s_rsum, 1)

            def post(i, kk):
                u = 4 * i + kk
                r = kk % RING
                dve.wait_ge(s_rsum, u + 1)
                dve.wait_ge(s_attn, u + 1)
                dve.wait_ge(s_xb, (2 * i + kk // 2 + 1))
                dve.scalar_tensor_tensor(x1[:, r], ps_o[:, 0:D], rsum[:, r:r + 1], x1[:, r], ALU.mult,
                                         ALU.add).then_inc(s_x1, 1)

            def ln2_stats(i, kk):
                u = 4 * i + kk
                dve.wait_ge(s_x1, u + 1)
                dve.bn_stats(st2[:], x1[:, kk % RING]).then_inc(s_st2, 1)

            def ln2_moments(i, kk):
                dve.wait_ge(s_st2, 4 * i + kk + 1)
                take_waits(2)
                dve.bn_aggr(mv2[:], st2[:]).then_inc(s_mv2, 1)

            def ln2_var(i, kk):
                dve.wait_ge(s_mv2, 4 * i + kk + 1)
                dve.tensor_scalar(ve2[:, 0:1], mv2[:, 1:2], LN_EPS, None, ALU.add)
                dve.tensor_scalar(ve2[:, 1:2], mv2[:, 1:2], 1.0 + RMS_EPS, RMS_EPS * LN_EPS, ALU.mult,
                                  ALU.add).then_inc(s_ve2, 1)

            def ln2_centre(i, kk):
                dve.scalar_tensor_tensor(xc[:], x1[:, kk % RING], mv2[:, 0:1], norm_rows[:], ALU.subtract,
                                         ALU.mult).then_inc(s_xc, 1)

            def ln2_norm(i, kk):
                u = 4 * i + kk
                dve.wait_ge(s_rs2, u + 1)
                wait(dve, s_base, u - 1)
                dve.tensor_scalar(y[:, kk % 2], x1[:, kk % RING], mv2[:, 0:1], rstd2[:, 0:1], ALU.subtract,
                                  ALU.mult).then_inc(s_y, 1)

            def rms_norm(i, kk):
                u = 4 * i + kk
                dve.wait_ge(s_xc, u + 1)
                wait(dve, s_rt, u - 1)
                wait(dve, s_keep, u - 1)
                dve.tensor_scalar(xn2[:, kk % 2], xc[:], rstd2[:, 1:2], None, ALU.mult).then_inc(s_xn2, 1)

            def take_logits(i, kk):
                u = 4 * i + kk
                dve.wait_ge(s_logits, u + 1)
                dve.tensor_copy(logits[:], ps_misc[:, 0:E]).then_inc(s_lg, 1)

            def best(i, kk):
                dve.wait_ge(s_lg, 4 * i + kk + 1)
                take_waits(3)
                dve.max(top[:], logits[:]).then_inc(s_top, 1)

            def best_index(i, kk):
                dve.wait_ge(s_top, 4 * i + kk + 1)
                take_waits(4)
                dve.max_index(top_i[:], top[:], logits[:]).then_inc(s_topi, 1)

            def best_difference(i, kk):
                wait(dve, s_e2, 4 * i + kk)
                dve.tensor_tensor(sdiff[:], top[:, 1:2], top[:, 0:1], ALU.subtract).then_inc(s_sd, 1)

            def best_number(i, kk):
                dve.wait_ge(s_topi, 4 * i + kk + 1)
                dve.tensor_copy(top_f[:, kk % 2], top_i[:, 0:2]).then_inc(s_topf, 1)

            def unit_gates(i, kk):
                return gate_all[:, bass.ds(4 * i + kk, 1)].rearrange("p a c -> p (a c)")

            def gates_sum(i, kk):
                dve.wait_ge(s_e2, 4 * i + kk + 1)
                dve.tensor_scalar(den[:], e2[:, kk % 2], 1.0, None, ALU.add).then_inc(s_den, 1)

            def gates_hot(i, kk):
                u = 4 * i + kk
                dve.wait_ge(s_topf, u + 1)
                for c in range(TOP_K):
                    dve.tensor_scalar(hot[:, c, bass.ds(u, 1)].rearrange("p a e -> p (a e)"), iota_f[:],
                                      top_f[:, kk % 2, c:c + 1], None, ALU.is_equal)

            def gates_first(i, kk):
                dve.wait_ge(s_den, 4 * i + kk + 1)
                dve.reciprocal(unit_gates(i, kk)[:, 0:1], den[:]).then_inc(s_w1, 1)

            def gates_second(i, kk):
                dve.wait_ge(s_w1, 4 * i + kk + 1)
                w = unit_gates(i, kk)
                dve.tensor_tensor(w[:, 1:2], w[:, 0:1], e2[:, kk % 2], ALU.mult).then_inc(s_gates, 1)

            def split_ctxt(i, j):
                b = 2 * i + j
                dve.wait_ge(s_ctxt_high, b + 1)
                wait(dve, s_scores, QT * (b - 1))
                dve.tensor_tensor(ctxt_low[:, j, 0:SK], ctxt_in[:], ctxt_high[:, j, 0:SK].bitcast(F32),
                                  ALU.subtract).then_inc(s_ctxt_low, 1)

            def split_up_weights(e):
                dve.wait_ge(s_wup_high, e + 1)
                dve.tensor_tensor(wup_low[:, bass.ds(e, 1)], wup_in[:].unsqueeze(1), wup_high[:, bass.ds(e, 1)].bitcast(F32),
                                  ALU.subtract).then_inc(s_wup_low, 1)

            def last_probs_t(i, k):
                u = 4 * i + k
                dve.wait_ge(s_turned, GROUPS * (u + 1))
                wait(dve, s_pv, u)
                dve.tensor_copy(probs_t[0:TAIL, (KT - 1) * P:KT * P],
                                ps_turn[0:TAIL, (GROUPS - 1) % 2, 0:P]).then_inc(s_pt_dve, 1)

            def slot(i, k):
                u = 4 * i + k
                nxt = (i, k // 2 + 1) if k < 2 else (i + 1, 0)
                following = (i, k + 1) if k < 3 else (i + 1, 0)
                prep = k % 2 == 0 and is_unit(u + 2)
                ln1 = k % 2 == 1 and is_unit(u + 3)
                ahead = (i + 1, k // 2)
                if prep:
                    split_ctxt(*nxt)
                if k == 3 and is_unit(u):
                    split_up_weights(i)
                if not prep and is_unit(u - 3):
                    gates_sum(i, k - 3)
                if ln1:
                    ln1_stats(*ahead)
                if not prep and is_unit(u - 3):
                    gates_hot(i, k - 3)
                    gates_first(i, k - 3)
                    gates_second(i, k - 3)
                if ln1:
                    ln1_moments(*ahead)
                if is_unit(u - 1):
                    post_sum(i, k - 1)
                if ln1:
                    ln1_var(*ahead)
                if is_unit(u - 1):
                    post(i, k - 1)
                if is_unit(u - 2):
                    take_logits(i, k - 2)
                if is_unit(u + 1):
                    maximum(*following)
                if is_unit(u - 2):
                    best(i, k - 2)
                if is_unit(u + 1):
                    bias_sum(*following)
                if is_unit(u - 2):
                    best_index(i, k - 2)
                if is_unit(u + 1):
                    bias(*following)
                if is_unit(u - 2):
                    best_difference(i, k - 2)
                if is_unit(u - 1):
                    ln2_stats(i, k - 1)
                if prep and is_unit(u - 3):
                    gates_sum(i, k - 3)
                if is_unit(u - 1):
                    ln2_moments(i, k - 1)
                if prep and is_unit(u - 3):
                    gates_hot(i, k - 3)
                if is_unit(u) and not prep:
                    last_probs_t(i, k)
                if is_unit(u - 1):
                    ln2_var(i, k - 1)
                if prep and is_unit(u - 3):
                    gates_first(i, k - 3)
                if is_unit(u - 1):
                    ln2_centre(i, k - 1)
                if prep and is_unit(u - 3):
                    gates_second(i, k - 3)
                if is_unit(u - 2):
                    best_number(i, k - 2)
                if ln1:
                    ln1_norm(*ahead)
                if prep:
                    prep_gt(*nxt)
                if is_unit(u) and prep:
                    last_probs_t(i, k)
                if is_unit(u - 1):
                    ln2_norm(i, k - 1)
                    rms_norm(i, k - 1)

            dve.wait_ge(s_mask, 16)
            dve.tensor_scalar(mbias_rows[:], mask_i[:], 0, MASKED, ALU.is_equal, ALU.mult).then_inc(s_mrows, 1)
            dve.wait_ge(s_iota, 1)
            def ln1(i, j):
                ln1_stats(i, j)
                ln1_moments(i, j)
                ln1_var(i, j)
                ln1_norm(i, j)

            ln1(0, 0)
            prep_gt(0, 0)
            split_ctxt(0, 0)
            maximum(0, 0)
            bias_sum(0, 0)
            bias(0, 0)
            ln1(0, 1)
            dve.wait_ge(s_consts, N_CONSTS)

            planned = [0]

            def then(instruction):
                planned[0] += 1
                instruction.then_inc(s_plan, 1)
                dve.wait_ge(s_plan, planned[0])

            def flat(t, g):
                return t[:, 0:E * GU[g]]

            def by_expert(t, g):
                return flat(t, g).rearrange("p (e u) -> p e u", e=E)

            def by_unit(t, g):
                return flat(t, g).rearrange("p (u e) -> p u e", e=E)

            def plan_ranks(g):
                n = E * GU[g]
                if g == 0:
                    dve.wait_ge(s_tables, 9)
                dve.wait_ge(s_rank, g + 1)
                dve.tensor_copy(flat(rank, g), ps_misc[:, 0:n])
                then(dve.tensor_copy(by_expert(total, g), ps_misc[:, n:2 * n].rearrange("p (u e) -> p e u", e=E)))
                then(dve.tensor_tensor_scan(flat(upto, g), keep[g][:].rearrange("p e u -> p (e u)"), flat(total, g), 0.0,
                                            ALU.mult, ALU.add))

            def plan_blocks(g):
                shape = [P, E, GU[g]]
                then(dve.tensor_tensor(by_expert(filled, g), by_expert(upto, g)[:, :, GU[g] - 1:GU[g]].broadcast_to(shape),
                                       rows128[:, 0:GU[g]].unsqueeze(1).broadcast_to(shape), ALU.is_gt))
                then(dve.tensor_reduce(blocks[:], by_expert(filled, g), AX.X, ALU.add))
                then(dve.tensor_tensor_scan(blocks_end[:], ones[:, 0:E], blocks[:], 0.0, ALU.mult, ALU.add))
                then(dve.tensor_tensor(blocks[:], blocks_end[:], blocks[:], ALU.subtract))

            def plan_owners(g):
                then(dve.tensor_tensor(past[:, 0:GB[g]], blocks_end[:].unsqueeze(1).broadcast_to([P, GB[g], E]),
                                       count_f[:, 0:GB[g]].unsqueeze(2).broadcast_to([P, GB[g], E]), ALU.is_le))
                then(dve.tensor_reduce(owner_f[:, 0:GB[g]], past[:, 0:GB[g]], AX.X, ALU.add))
                dve.tensor_scalar(owner[:, FIRST_BLOCK[g]:FIRST_BLOCK[g] + GB[g]], owner_f[:, 0:GB[g]], E - 1.0, None,
                                  ALU.min).then_inc(s_owner, 1)

            def plan_places(g):
                us = slice(FIRST_UNIT[g], FIRST_UNIT[g] + GU[g])
                then(dve.tensor_tensor(flat(first, g), flat(upto, g), flat(total, g), ALU.subtract))
                then(dve.scalar_tensor_tensor(by_expert(first, g), blocks[:].unsqueeze(2).broadcast_to([P, E, GU[g]]), float(P),
                                              by_expert(first, g), ALU.mult, ALU.add))
                then(dve.tensor_tensor(by_unit(spot, g), by_unit(rank, g), by_expert(first, g).rearrange("p e u -> p u e"),
                                       ALU.add))
                for c in range(TOP_K):
                    last = dve.tensor_tensor(by_unit(spot_k[:, c], g), hot[:, c, us], by_unit(spot, g), ALU.mult)
                then(last)
                for c in range(TOP_K):
                    last = dve.tensor_reduce(place_f[:, c, 0:GU[g]], by_unit(spot_k[:, c], g), AX.X, ALU.add)
                then(last)
                dve.tensor_copy(place[:, :, us], place_f[:, :, 0:GU[g]]).then_inc(s_place, 1)

            def split_block(i, k):
                m = SB * i + k
                dve.wait_ge(s_xt_high, m + 1)
                wait(dve, s_up, m - 1)
                dve.tensor_tensor(xt_low[:, k % 2], ps[:, 0, 0:P], xt_high[:, k % 2].bitcast(F32),
                                  ALU.subtract).then_inc(s_xt_low, 1)

            def step(i, k):
                m = SB * i + k
                if is_block(m + 1):
                    split_block(*shift(i, k, 1, SB))
                if is_block(m):
                    dve.wait_ge(s_th, m + 1)
                    dve.scalar_tensor_tensor(sg[:, k % 2], th[:, k % 2], 1.0, ps[:, 2 + k % 2, H:H2], ALU.add,
                                             ALU.mult).then_inc(s_sg, 1)
                    dve.wait_ge(s_sg, m + 1)
                    wait(dve, s_ht, m - 1)
                    dve.scalar_tensor_tensor(hid[:, k % 2], sg[:, k % 2], 0.5, ps[:, 2 + k % 2, 0:H], ALU.mult,
                                             ALU.mult).then_inc(s_h, 1)

            first_plan = {0: [plan_ranks, plan_blocks], 1: [plan_places], 2: [plan_owners]}
            second_plan = {3: [plan_ranks], 4: [plan_blocks], 5: [plan_places], 6: [plan_owners]}
            run(dve, slot, first_plan, lambda: split_block(0, 0), step, second_plan)
            assert planned[0] == GROUPS_D * PLAN_STEPS

            dve.wait_ge(s_base, UNITS)
            for u in range(UNITS):
                dve.wait_ge(s_got[u // GOT], 16 * TOP_K * GOT)
                dve.scalar_tensor_tensor(base_all[:, u], got[:, u % ROOM, 0], gate_all[:, u, 0:1], base_all[:, u], ALU.mult,
                                         ALU.add).then_inc(s_part, 1)
                dve.wait_ge(s_part, u + 1)
                dve.scalar_tensor_tensor(base_all[:, u], got[:, u % ROOM, 1], gate_all[:, u, 1:2], base_all[:, u], ALU.mult,
                                         ALU.add).then_inc(s_final, 1)

        @block.tensor
        def _(pe):
            pe.wait_ge(s_consts_qk, N_CONSTS)
            pe.wait_ge(s_pad, 2)
            pe.wait_ge(s_ident, 1)

            def prep_xt(i, j, routed):
                b = 2 * i + j
                pe.wait_ge(s_xn1, b + 1)
                wait(pe, s_lg, routed)
                wait(pe, s_gtc, b)
                for t in range(QT):
                    last = pe.transpose(ps_misc[:, t * P:(t + 1) * P], xn1[:, j, t], ident[:])
                last.then_inc(s_xt, 1)

            def prep_qt(i, j):
                b = 2 * i + j
                pe.wait_ge(s_xtc, b + 1)
                pe.matmul(ps_misc[:, 0:SQ], wq_sb[:], xt_sb[:], start=True, stop=True).then_inc(s_qt, 1)

            def prep_gt(i, j):
                b = 2 * i + j
                pe.wait_ge(s_qtc, b + 1)
                pe.matmul(ps_misc[:, 0:SQ], wkt_sb[:], qt_sb[:], start=True, stop=True)
                for t in range(QT):
                    last = pe.matmul(ps_misc[:, SQ + t:SQ + t + 1], qt_sb[:, t * P:(t + 1) * P], bk_col[:],
                                     start=True, stop=True)
                last.then_inc(s_gt, 1)

            def score(i, k):
                u = 4 * i + k
                j = k // 2
                pe.wait_ge(s_gtc, 2 * i + j + 1)
                pe.wait_ge(s_ctxt_low, 2 * i + j + 1)
                wait(pe, s_max, u)
                for c in range(0, SKE, BANK):
                    n = min(BANK, SKE - c)
                    products = ((gt_high, ctxt_high), (gt_high, ctxt_low), (gt_low, ctxt_high))
                    for m, (queries, keys) in enumerate(products):
                        last = pe.matmul(ps_scores[:, c:c + n], queries[:, j, (k % 2) * P:(k % 2 + 1) * P],
                                         keys[:, j, c:c + n], start=m == 0, stop=m == len(products) - 1)
                last.then_inc(s_scores, 1)

            def turn(i, k, g):
                u = 4 * i + k
                if g == 0:
                    pe.wait_ge(s_exp, u + 1)
                if g < 2:
                    wait(pe, *((s_pt_act, 3 * u) if g == 0 else (s_pt_dve, u)))
                else:
                    pe.wait_ge(s_pt_act, 3 * u + g - 1)
                for t in range(4 * g, min(4 * g + 4, KT)):
                    n = batch_part(t)
                    last = pe.transpose(ps_turn[0:n, g % 2, (t - 4 * g) * P:(t - 4 * g + 1) * P],
                                        probs[:, k % 2, t * P:t * P + n], ident[:])
                last.then_inc(s_turned, 1)

            def times_ctx(i, k, g):
                u = 4 * i + k
                j = k // 2
                if g == 0:
                    pe.wait_ge(s_ctx[j], 32 * (i + 1))
                    wait(pe, s_x1, u)
                if g < GROUPS - 1:
                    pe.wait_ge(s_pt_act, 3 * u + g + 1)
                else:
                    pe.wait_ge(s_pt_dve, u + 1)
                for t in range(4 * g, min(4 * g + 4, KT)):
                    n = batch_part(t)
                    last = pe.matmul(ps_o[:, 0:P], ctx_sb[0:n, j, t], probs_t[0:n, t * P:(t + 1) * P],
                                     start=t == 0, stop=t == KT - 1)
                if g == GROUPS - 1:
                    last.then_inc(s_pv, 1)

            def route(i, kk):
                pe.wait_ge(s_rtc, 4 * i + kk + 1)
                pe.matmul(ps_misc[:, 0:E], xnt[:, kk % 2], wr_sb[:], start=True, stop=True).then_inc(s_logits, 1)

            def slot(i, k):
                u = 4 * i + k
                nxt = (i, k // 2 + 1) if k < 2 else (i + 1, 0)
                prep = k % 2 == 0 and is_unit(u + 2)
                if is_unit(u + 1):
                    score(*((i, k + 1) if k < 3 else (i + 1, 0)))
                if is_unit(u - 2):
                    pe.wait_ge(s_xn2, u - 1)
                    wait(pe, s_lg, u - 2)
                    if k % 2 == 1 and is_unit(u + 1):
                        pe.wait_ge(s_gtc, (2 * i + k // 2 + 2))
                    pe.transpose(ps_misc[:, 0:P], xn2[:, (k - 2) % 2], ident[:]).then_inc(s_rt, 1)
                if is_unit(u - 1):
                    pe.wait_ge(s_ot, u)
                    pe.matmul(ps_o[:, 0:D], o_t[:, (k - 1) % 2], wv_sb[:], start=True, stop=True).then_inc(s_attn, 1)
                if is_unit(u):
                    turn(i, k, 0)
                if is_unit(u - 2):
                    route(i, k - 2)
                if is_unit(u):
                    turn(i, k, 1)
                if prep:
                    prep_xt(*nxt, u - 1)
                if is_unit(u):
                    times_ctx(i, k, 0)
                if prep:
                    prep_qt(*nxt)
                if is_unit(u):
                    turn(i, k, 2)
                    times_ctx(i, k, 1)
                if prep:
                    prep_gt(*nxt)
                if is_unit(u):
                    turn(i, k, 3)
                    times_ctx(i, k, 2)
                    times_ctx(i, k, 3)

            prep_xt(0, 0, 0)
            prep_qt(0, 0)
            prep_gt(0, 0)
            score(0, 0)
            pe.wait_ge(s_consts, N_CONSTS)

            def rank_rows(g):
                units = FIRST_UNIT[g] + GU[g]
                pe.wait_ge(s_gates, units)
                pe.wait_ge(s_lg, min(units + 1, UNITS))
                pe.wait_ge(s_rtc, min(units + 1, UNITS))
                for n, table in enumerate((before, ones)):
                    for c in range(TOP_K):
                        rows = hot[:, c, FIRST_UNIT[g]:units].rearrange("p u e -> p (u e)")
                        last = pe.matmul(ps_misc[:, n * GU[g] * E:(n + 1) * GU[g] * E], table[:], rows, start=c == 0,
                                         stop=c == TOP_K - 1)
                last.then_inc(s_rank, 1)
                if g == 0:
                    pe.wait_ge(s_plan, 1)

            def turn_block(i, k):
                m = SB * i + k
                if k % CH == 0:
                    pe.wait_ge(s_blk[k // CH], 16 * (i + 1))
                wait(pe, s_xt_low, m)
                pe.transpose(ps[:, 0, 0:P], blk_x[:, k // CH, k % CH], ident[:]).then_inc(s_bxt, 1)

            owner_regs = [pe.alloc_register(f"owner{k}") for k in range(SB)]

            def load_owners(i, k):
                pe.load(owner_regs[k:k + CH], owner[0:1, bass.ds(SB * i + k, CH)])

            def expert(k):
                return pe.snap(owner_regs[k], min_val=0, max_val=E - 1)

            def step(i, k):
                m = SB * i + k
                if k == 1 and not isinstance(i, int):
                    pe.wait_ge(s_owner, GROUPS_D)
                if is_block(m + 1):
                    turn_block(*shift(i, k, 1, SB))
                if is_block(m):
                    e = expert(k)
                    pe.wait_ge(s_xt_low, m + 1)
                    wait(pe, s_h, m - 1)
                    products = ((xt_high, wup_high), (xt_high, wup_low), (xt_low, wup_high))
                    for n, (rows, weights) in enumerate(products):
                        last = pe.matmul(ps[:, 2 + k % 2], rows[:, k % 2],
                                         weights[:, bass.ds(e, 1)].rearrange("p a h -> p (a h)"), start=n == 0,
                                         stop=n == len(products) - 1)
                    last.then_inc(s_up, 1)
                    if k % CH == CH - 1 and is_block(m + 1):
                        load_owners(*shift(i, k, 1, SB))
                if is_block(m - 2):
                    pe.wait_ge(s_h, m - 1)
                    wait(pe, s_htc, m - 3)
                    for c in range(HC):
                        last = pe.transpose(ps[:, 4 + k % 2, c * P:(c + 1) * P], hid[:, k % 2, c * P:(c + 1) * P], ident[:])
                    last.then_inc(s_ht, 1)
                if is_block(m - 3):
                    e = expert((k - 3) % SB)
                    pe.wait_ge(s_htc, m - 2)
                    wait(pe, s_y2, m - 4)
                    for c in range(HC):
                        last = pe.matmul(ps[:, (1, 6)[k % 2], 0:D], hid_t[:, (k - 3) % 2, c * P:(c + 1) * P],
                                         wdn_sb[:, bass.ds(e, 1), c].rearrange("p a d -> p (a d)"),
                                         start=c == 0, stop=c == HC - 1)
                    last.then_inc(s_down, 1)

            def before_steps():
                pe.wait_ge(s_wdn, 16 * E)
                pe.wait_ge(s_wup_low, E)
                pe.wait_ge(s_max, UNITS)
                pe.wait_ge(s_pt_dve, UNITS)
                pe.wait_ge(s_pt_act, 3 * UNITS)
                pe.wait_ge(s_owner, 1)
                load_owners(0, 0)
                turn_block(0, 0)

            run(pe, slot, {0: [rank_rows]}, before_steps, step, {2: [rank_rows]})


def kernel(x, ctx_1024, mask_BxS2_ik0, L0_xattn_Wq, L0_xattn_bq, L0_xattn_Wk, L0_xattn_bk, L0_xattn_Wv,
           L0_xattn_bv, L0_ffn_norm_scale, L0_ffn_w_router, L0_ffn_w_up, L0_ffn_w_down):
    import numpy as np
    import concourse.bacc as bacc
    from concourse.bass_utils import run_bass_kernel_spmd

    def turned(a, *axes):
        return np.ascontiguousarray(np.asarray(a).transpose(*axes))

    arrays = {
        "x": np.ascontiguousarray(x),
        "ctx_rows": np.ascontiguousarray(ctx_1024),
        "ctx_cols": turned(ctx_1024, 0, 2, 1),
        "mask": np.ascontiguousarray(mask_BxS2_ik0),
        "wq": np.ascontiguousarray(L0_xattn_Wq),
        "wk_t": turned(L0_xattn_Wk, 1, 0),
        "wv": np.ascontiguousarray(L0_xattn_Wv),
        "bq": np.asarray(L0_xattn_bq).reshape(-1, 1),
        "bk": np.asarray(L0_xattn_bk).reshape(-1, 1),
        "bv": np.ascontiguousarray(L0_xattn_bv),
        "norm_scale": np.ascontiguousarray(L0_ffn_norm_scale),
        "w_router_t": turned(L0_ffn_w_router, 1, 0),
        "w_up_t": turned(L0_ffn_w_up, 0, 2, 1),
        "w_down_t": turned(L0_ffn_w_down, 0, 2, 1),
    }
    nc = bacc.Bacc("TRN2", target_bir_lowering=False, num_devices=1)
    aps = [nc.dram_tensor(n, a.shape, mybir.dt.from_np(a.dtype), kind="ExternalInput").ap() for n, a in arrays.items()]
    out = nc.dram_tensor("out", arrays["x"].shape, F32, kind="ExternalOutput").ap()
    xattn_moe(nc, *aps, out)
    result = run_bass_kernel_spmd(nc, [arrays], core_ids=[0])
    return result.results[0]["out"]
```
